# Optimizing a Trainium2 kernel written in Bass

```python
import numpy as np
import jax
import jax.numpy as jnp

def _softmax(x, axis=-1):
    return jax.nn.softmax(x, axis=axis)

def _gelu(x):
    return jax.nn.gelu(x, approximate=True)

def _silu(x):
    return jax.nn.silu(x)

def _sigmoid(x):
    return jax.nn.sigmoid(x)

def _layernorm(x, axis=-1, eps=1e-05):
    m = jnp.mean(x, axis=axis, keepdims=True)
    v = jnp.var(x, axis=axis, keepdims=True)
    return (x - m) / jnp.sqrt(v + eps)

def _scatter_add(tgt, idx, src, axis=0):
    return tgt.at[idx].add(src)

def _segment_sum(src, seg, n):
    return jax.ops.segment_sum(src, seg, n)
kernel_name = 'mk_audio_tower_d1_tok_audfeat512_r4_c9ef6a'

def setup_inputs(seed: int=0):
    np.random.seed(seed)
    _w = jnp.asarray

    def _rec_inputs():
        import jax
        import jax.numpy as jnp
        _rk = jax.random.key(seed)
        x = -0.0003702 + 0.999946 * jax.random.normal(jax.random.fold_in(_rk, 1), (32, 375, 128), jnp.float32)
        return x
    x = _rec_inputs()

    def _L0_tok_setup():
        import jax, jax.numpy as jnp
        import numpy as np
        CONTEXT_LEN = 3
        SUBSAMPLING = 1
        key = jax.random.key(seed)
        k1, k2, k3 = jax.random.split(key, 3)
        mb, N, D = (32, 250, 128)
        out_features = 128
        inp = jax.random.normal(k1, (mb, N, D), dtype=jnp.float32)
        fan_in = D * CONTEXT_LEN
        weight = jax.random.normal(k2, (out_features, fan_in), dtype=jnp.float32) / np.sqrt(fan_in)
        bias = jax.random.normal(k3, (out_features,), dtype=jnp.float32) * 0.01
        return {'input': inp, 'weight': weight, 'bias': bias}
    _L0_tok_all = _L0_tok_setup()
    _L0_tok_in = {k: v for k, v in _L0_tok_all.items() if k in ('weight', 'bias')}
    del _L0_tok_all

    def _L0_attn_setup():
        import jax, jax.numpy as jnp
        import numpy as np
        import math
        D_MODEL = 128
        SLOPE = 0.5
        key = jax.random.key(seed)
        k1, k2, k3, k4 = jax.random.split(key, 4)
        B, S, D = (4, 1024, D_MODEL)
        x = jax.random.normal(k1, (B, S, D), dtype=jnp.float32)
        lim = 1.0 / math.sqrt(D)
        W_qk = jax.random.uniform(k2, (D, D), jnp.float32, -lim, lim)
        W_v = jax.random.uniform(k3, (D, D), jnp.float32, -lim, lim)
        b_v = jax.random.uniform(k4, (D,), jnp.float32, -lim, lim)
        return {'x': x, 'W_qk': W_qk, 'W_v': W_v, 'b_v': b_v}
    _L0_attn_all = _L0_attn_setup()
    _L0_attn_in = {k: v for k, v in _L0_attn_all.items() if k in ('W_qk', 'W_v', 'b_v')}
    del _L0_attn_all

    def _L0_ffn_setup():
        import jax, jax.numpy as jnp
        import numpy as np
        B, S, D = (8, 2048, 128)
        E, DFF = (16, 128)
        CAPACITY = 2
        key = jax.random.key(seed)
        ks = jax.random.split(key, 4)
        x = jax.random.normal(ks[0], (B, S, D), dtype=jnp.float32)
        gate_weight = jax.random.normal(ks[1], (D, E), dtype=jnp.float32) * 0.006
        w1 = jax.random.normal(ks[2], (E, D, DFF), dtype=jnp.float32) * 0.02
        b1 = jnp.zeros((E, DFF), dtype=jnp.float32)
        w2 = jax.random.normal(ks[3], (E, DFF, D), dtype=jnp.float32) * 0.02
        b2 = jnp.zeros((E, D), dtype=jnp.float32)
        return {'x': x, 'gate_weight': gate_weight, 'w1': w1, 'b1': b1, 'w2': w2, 'b2': b2}
    _L0_ffn_all = _L0_ffn_setup()
    _L0_ffn_in = {k: v for k, v in _L0_ffn_all.items() if k in ('gate_weight', 'w1', 'b1', 'w2', 'b2')}
    del _L0_ffn_all
    return {'x': x, 'L0_tok_weight': _L0_tok_in['weight'], 'L0_tok_bias': _L0_tok_in['bias'], 'L0_attn_W_qk': _L0_attn_in['W_qk'], 'L0_attn_W_v': _L0_attn_in['W_v'], 'L0_attn_b_v': _L0_attn_in['b_v'], 'L0_ffn_gate_weight': _L0_ffn_in['gate_weight'], 'L0_ffn_w1': _L0_ffn_in['w1'], 'L0_ffn_b1': _L0_ffn_in['b1'], 'L0_ffn_w2': _L0_ffn_in['w2'], 'L0_ffn_b2': _L0_ffn_in['b2']}

def reference(x, L0_tok_weight, L0_tok_bias, L0_attn_W_qk, L0_attn_W_v, L0_attn_b_v, L0_ffn_gate_weight, L0_ffn_w1, L0_ffn_b1, L0_ffn_w2, L0_ffn_b2):
    import jax
    import jax.numpy as jnp

    def _L0_tok_ref(input, weight, bias):
        import jax, jax.numpy as jnp
        import numpy as np
        CONTEXT_LEN = 3
        SUBSAMPLING = 1
        mb, N, D = input.shape
        l = CONTEXT_LEN
        expected_N = N - l + 1
        padded = jnp.concatenate([jax.lax.dynamic_slice_in_dim(input, i, expected_N, axis=1) for i in range(l)], axis=-1)
        if SUBSAMPLING > 1:
            padded = padded[:, ::SUBSAMPLING, :]
        x = jnp.einsum('btf,of->bto', padded, weight) + bias
        return jax.nn.relu(x)

    def _L0_attn_ref(x, W_qk, W_v, b_v):
        import jax, jax.numpy as jnp
        import numpy as np
        import math
        D_MODEL = 128
        SLOPE = 0.5
        B, S, D = x.shape
        scale = 1.0 / math.sqrt(D)
        scores = jnp.einsum('bid,de,bje->bij', x, W_qk, x) * scale
        i = jnp.arange(S, dtype=x.dtype)[:, None]
        j = jnp.arange(S, dtype=x.dtype)[None, :]
        scores = scores + (j - i) * jnp.asarray(SLOPE, x.dtype)
        causal = j > i
        scores = jnp.where(causal, -jnp.inf, scores)
        attn = jax.nn.softmax(scores, axis=-1)
        v = jnp.einsum('bjd,ed->bje', x, W_v) + b_v
        return jnp.einsum('bij,bje->bie', attn, v)

    def _L0_ffn_ref(x, gate_weight, w1, b1, w2, b2):
        import jax, jax.numpy as jnp
        import numpy as np
        B, S, D = (8, 2048, 128)
        E, DFF = (16, 128)
        CAPACITY = 2
        Bx, Sx, Dx = x.shape
        num_experts = gate_weight.shape[1]
        k = Sx // num_experts * CAPACITY
        logits = jnp.einsum('bsd,de->bse', x, gate_weight)
        affinity = jax.nn.softmax(logits, axis=-1).transpose(0, 2, 1)
        gating, index = jax.lax.top_k(affinity, k)
        x_in = jnp.take_along_axis(x[:, None, :, :], index[..., None], axis=2)
        h = jax.nn.gelu(jnp.einsum('bekd,edh->bekh', x_in, w1) + b1[None, :, None, :])
        x_e = jnp.einsum('bekh,ehd->bekd', h, w2) + b2[None, :, None, :]
        weighted = gating[..., None] * x_e
        out = jnp.zeros_like(x)
        idx_flat = index.reshape(Bx, num_experts * k)
        vals_flat = weighted.reshape(Bx, num_experts * k, Dx)
        out = out.at[jnp.arange(Bx)[:, None], idx_flat].add(vals_flat)
        return out
    h = _L0_tok_ref(x, L0_tok_weight, L0_tok_bias)
    h = h + _L0_attn_ref(_layernorm(h, axis=-1), L0_attn_W_qk, L0_attn_W_v, L0_attn_b_v)
    h = h + _L0_ffn_ref(_layernorm(h, axis=-1), L0_ffn_gate_weight, L0_ffn_w1, L0_ffn_b1, L0_ffn_w2, L0_ffn_b2)
    return h

_drawn_inputs = setup_inputs


def setup_inputs(seed=0):
    import zlib

    import numpy as np

    out = dict(_drawn_inputs(seed))
    spreads = {'L0_ffn_b1': (0.0, 0.8), 'L0_ffn_b2': (0.0, 0.645)}
    factors = {'L0_tok_bias': 4.69, 'L0_ffn_gate_weight': 4.645, 'L0_ffn_w1': 8.0, 'L0_ffn_w2': 8.0}
    for name, (base, spread) in spreads.items():
        noise = np.random.default_rng([zlib.crc32(name.encode()), seed]).standard_normal(out[name].shape)
        drawn = base * np.exp(spread * noise) if base else spread * noise
        out[name] = jnp.asarray(drawn.astype(out[name].dtype))
    for name, factor in factors.items():
        out[name] = (out[name] * factor).astype(out[name].dtype)
    return out
```

```python
from contextlib import ExitStack

import concourse.bass as bass
from concourse import mybir

F32 = mybir.dt.float32
I32 = mybir.dt.int32
U32 = mybir.dt.uint32
ALU = mybir.AluOpType
ACT = mybir.ActivationFunctionType
AX_X = mybir.AxisListType.X

P = 128
NEG = -3.0e38


def audio_tower_block(nc, x, w_tok, b_tok, w_qk, w_v, b_v, w_gate, w1, b1, w2, b2, out, xn2_rows, slots_dram):
    B, NTOK, D = x.shape
    CTX = w_tok.shape[1] // D
    S = NTOK - CTX + 1
    E = w_gate.shape[1]
    CAP = S // E * 2
    TILES = -(-S // P)
    SP = TILES * P
    LAST = S - (TILES - 1) * P
    LASTX = NTOK - (TILES - 1) * P
    G = P // E
    GROUPS = B // G
    SLOTS = G * CAP
    ROUNDS = -(-CAP // 8)
    LAST_SLOTS = SLOTS - 2 * P
    PAIRS = E // 2
    NF = GROUPS * PAIRS
    SCALE = float(D) ** -0.5
    EPS = 1e-5
    SLOPE = 0.5
    GELU_C = 0.044715
    GELU_S = 0.7978845608028654
    RSQRT_MAGIC = 1597463007.0
    assert TILES == 3 and D == P and G * E == P and SLOTS <= 3 * P and G == PAIRS
    XCOLS = (TILES - 1) * P + P + CTX - 1
    ROWS = [P, P, LAST_SLOTS]
    SW = [P * (t + 1) for t in range(TILES)]
    SO = [0, P, 3 * P]

    out_rows = out.rearrange("b s d -> (b s) d")
    x_rows = x.rearrange("b s d -> (b s) d")

    with ExitStack() as ctx:
        def sb(name, shape, dt=F32):
            return ctx.enter_context(nc.sbuf_tensor(name, shape, dt))

        def sem(name):
            return ctx.enter_context(nc.semaphore(name))

        ident = sb("ident", [P, P])
        dist_bias = sb("dist_bias", [P, TILES, SP])
        w_tok_raw = sb("w_tok_raw", [P, CTX * D])
        w_v_raw = sb("w_v_raw", [P, D])
        b1_raw = sb("b1_raw", [E, D])
        w_tokT = sb("w_tokT", [P, CTX * D])
        w_vT = sb("w_vT", [P, D])
        b1T = sb("b1T", [P, E])
        w_qk_sb = sb("w_qk_sb", [P, D])
        w_gate_sb = sb("w_gate_sb", [P, E])
        b_tok_rep = sb("b_tok_rep", [P, D])
        b_v_rep = sb("b_v_rep", [P, D])
        slot_base = sb("slot_base", [P, 1])
        slot_base_i = sb("slot_base_i", [P, 1], I32)
        xs = sb("xs", [P, TILES, D])
        xT = sb("xT", [P, XCOLS])
        hpre = sb("hpre", [P, TILES, D])
        h = sb("h", [P, TILES, D])
        xn = sb("xn", [P, TILES, D])
        hres = sb("hres", [P, TILES, D])
        xnT = sb("xnT", [P, SP])
        qT = sb("qT", [P, SP])
        v = sb("v", [P, TILES, D])
        probs = sb("probs", [P, 6 * P])
        row_max = sb("row_max", [P, TILES])
        neg_max = sb("neg_max", [P, TILES])
        row_sum = sb("row_sum", [P, TILES])
        row_inv = sb("row_inv", [P, TILES])
        probsT = sb("probsT", [P, 6, P])
        h2 = sb("h2", [P, TILES, D])
        xn2 = sb("xn2", [P, TILES, D])
        ln = [{n: sb(f"ln{i}_{n}", [P, TILES, k]) for n, k in
               (("stats", 6), ("mv", 2), ("var", 1), ("y", 1), ("t", 1))} for i in range(2)]
        xn2T = sb("xn2T", [P, SP])
        r_max = sb("r_max", [P, TILES, 1])
        r_exp = sb("r_exp", [P, TILES, E])
        r_sum = sb("r_sum", [P, TILES, 1])
        aff = sb("aff", [P, TILES, E, G])
        affT = sb("affT", [P, S])
        top_val = sb("top_val", [P, 8 * ROUNDS])
        top_idx = sb("top_idx", [P, 8 * ROUNDS], U32)
        slots = sb("slots", [P, 2, CAP])
        slot_rows = sb("slot_rows", [2 * E, SLOTS])
        tab_idx = sb("tab_idx", [P, TILES, E], I32)
        tab_gate = sb("tab_gate", [P, TILES, E])
        gather_idx = sb("gather_idx", [P, TILES, 2], I32)
        scatter_idx = sb("scatter_idx", [P, TILES, 2], I32)
        gate = sb("gate", [P, TILES, 2])
        half_b1 = sb("half_b1", [P, 2])
        w1_sb = [sb(f"w1_{i}", [P, D]) for i in "ab"]
        w2_sb = [sb(f"w2_{i}", [P, D]) for i in "ab"]
        b2_rep = [sb(f"b2_rep_{i}", [P, D]) for i in "ab"]
        xg = [sb(f"xg_{i}", [P, TILES, D]) for i in "ab"]
        y = [sb(f"y_{i}", [P, TILES, D]) for i in "ab"]
        xgT = sb("xgT", [P, SLOTS])
        u = sb("u", [P, SLOTS])
        u_sq = sb("u_sq", [P, SLOTS])
        gelu_in = sb("gelu_in", [P, SLOTS])
        tanh_out = sb("tanh_out", [P, SLOTS])
        hidT = sb("hidT", [P, SLOTS])

        ps = [ctx.enter_context(nc.psum_tensor(f"bank{i}", [P, 512], F32)) for i in range(8)]
        ps_x = ps[1]
        ps_q = ps[0]
        ps_v = ps[2]
        ps_s = [ps[3], ps[4]]
        ps_g = ps[5]
        ps_u = ps[6]
        ps_y = ps[7]

        consts_loaded = sem("consts_loaded")
        pool_setup = sem("pool_setup")
        vec_setup = sem("vec_setup")
        weights_transposed = sem("weights_transposed")
        weights_ready = sem("weights_ready")
        x_loaded = sem("x_loaded")
        x_transposed = sem("x_transposed")
        xT_copied = sem("xT_copied")
        conv_done = sem("conv_done")
        conv_added = sem("conv_added")
        relu_done = sem("relu_done")
        x_vec = sem("x_vec")
        xn_ready = sem("xn_ready")
        xn_transposed = sem("xn_transposed")
        xnT_copied = sem("xnT_copied")
        q_done = sem("q_done")
        q_copied = sem("q_copied")
        v_done = sem("v_done")
        v_added = sem("v_added")
        s_done = sem("s_done")
        y_vec = sem("y_vec")
        max_ready = sem("max_ready")
        exp_done = sem("exp_done")
        pT_done = sem("pT_done")
        pT_copied = sem("pT_copied")
        pv_done = sem("pv_done")
        attn_added = sem("attn_added")
        xn2_ready = sem("xn2_ready")
        rows_stored = sem("rows_stored")
        xn2_transposed = sem("xn2_transposed")
        xn2T_copied = sem("xn2T_copied")
        logits_done = sem("logits_done")
        logits_read = sem("logits_read")
        r_exp_done = sem("r_exp_done")
        r_vec = sem("r_vec")
        aff_ready = sem("aff_ready")
        aff_transposed = sem("aff_transposed")
        t_vec = sem("t_vec")
        slots_ready = sem("slots_ready")
        slots_stored = sem("slots_stored")
        slots_loaded = sem("slots_loaded")
        tab_transposed = sem("tab_transposed")
        tab_ready = sem("tab_ready")
        gather_idx_ready = sem("gather_idx_ready")
        pair_ready = sem("pair_ready")
        table_ready = sem("table_ready")
        gathered = [sem(f"gathered_{i}") for i in "ab"]
        scattered = [sem(f"scattered_{i}") for i in "ab"]
        w1_loaded = [sem(f"w1_loaded_{i}") for i in "ab"]
        w2_loaded = [sem(f"w2_loaded_{i}") for i in "ab"]
        b2_loaded = [sem(f"b2_loaded_{i}") for i in "ab"]
        xg_transposed = sem("xg_transposed")
        xgT_copied = sem("xgT_copied")
        ffn1_done = sem("ffn1_done")
        u_copied = sem("u_copied")
        u_squared = sem("u_squared")
        gelu_in_ready = sem("gelu_in_ready")
        tanh_done = sem("tanh_done")
        hid_ready = sem("hid_ready")
        ffn2_done = sem("ffn2_done")
        y_added = sem("y_added")
        y_ready = sem("y_ready")

        spacer = [sem("spacer_pool"), sem("spacer_vec")]

        block = ctx.enter_context(nc.Block())

        def steps(eng, step):
            last = B + 1 + PAIRS

            def one(j, lo):
                step(j if lo < B else None,
                     j - 1 if 1 <= lo <= B else None,
                     j - 2 if 2 <= lo <= B + 1 else None,
                     (lo - 2) % G,
                     (lo - 2) // G,
                     (lo - 9) // G if 9 <= lo <= B + 1 and (lo - 9) % G == 0 else None,
                     j - 10 if lo >= 10 else None,
                     (lo - 10) % PAIRS,
                     (lo - 10) // PAIRS,
                     j - lo,
                     9 <= lo < last)

            for lo, hi in ((0, 1), (1, 2), (2, 9), (9, 10), (10, 11), (11, 17), (17, 18), (18, 25), (25, 26),
                           (26, 31), (31, 32), (32, 33), (33, 34), (34, last), (last, last + 1)):
                if hi - lo == 1:
                    one(lo, lo)
                else:
                    with eng.Fori(lo, hi) as j:
                        one(j, lo)

        def alone(eng):
            eng.sem_inc(spacer[0 if eng is nc.gpsimd else 1], 1)

        @block.sync
        def _(sp):
            for dst, src in ((w_tok_raw[:, :], w_tok), (w_v_raw[:, :], w_v), (b1_raw[:, :], b1),
                             (w_qk_sb[:, :], w_qk), (w_gate_sb[:, :], w_gate),
                             (b_tok_rep[:, :], b_tok.rearrange("(a d) -> a d", a=1).to_broadcast([P, D])),
                             (b_v_rep[:, :], b_v.rearrange("(a d) -> a d", a=1).to_broadcast([P, D]))):
                sp.dma_start(dst, src).then_inc(consts_loaded, 16)

            def load_x(b):
                r = b * NTOK
                sp.dma_start(xs[:, 0:2, :], x_rows[bass.ds(r, 2 * P), :].rearrange("(t p) d -> p t d", p=P)) \
                    .then_inc(x_loaded, 16)
                sp.dma_start(xs[0:LASTX, 2, :], x_rows[bass.ds(r + 2 * P, LASTX), :]).then_inc(x_loaded, 16)

            def store_rows(b, in_group, g):
                for dst, r, src in ((out_rows, b * S, h2), (xn2_rows[g], in_group * S, xn2)):
                    sp.dma_start(dst[bass.ds(r, 2 * P), :].rearrange("(t p) d -> p t d", p=P), src[:, 0:2, :]) \
                        .then_inc(rows_stored, 16)
                    sp.dma_start(dst[bass.ds(r + 2 * P, LAST), :], src[0:LAST, 2, :]).then_inc(rows_stored, 16)

            def expert(t, e):
                return t[bass.ds(e, 1)]

            load_x(0)

            def step(xb, yb, rb, k, rg, t, f, fk, fg, dj, prep):
                if rb is not None:
                    sp.wait_ge(xn2_ready, rb + 1)
                    if not (isinstance(rb, int) and rb == 0):
                        sp.wait_ge(rows_stored, rb * 64)
                    store_rows(rb, dj + k, rg)
                nk = (fk + 1) % PAIRS if f is not None else 0

                def load(which, half, free):
                    e = (dj + nk) * 2 + half
                    if f is not None:
                        sp.wait_ge(free, f * 2 + half + 1)
                    if which == "w1":
                        sp.dma_start(w1_sb[half][:, :], expert(w1, e).rearrange("a d n -> (a d) n")) \
                            .then_inc(w1_loaded[half], 16)
                    elif which == "w2":
                        sp.dma_start(w2_sb[half][:, :], expert(w2, e).rearrange("a d n -> (a d) n")) \
                            .then_inc(w2_loaded[half], 16)
                    else:
                        sp.dma_start(b2_rep[half][:, :], expert(b2, e).to_broadcast([P, D])) \
                            .then_inc(b2_loaded[half], 16)

                if prep:
                    load("w1", 0, ffn1_done)
                if xb is not None and not (isinstance(xb, int) and xb == B - 1):
                    sp.wait_ge(x_transposed, xb + 1)
                    load_x(xb + 1)
                if prep:
                    load("w1", 1, ffn1_done)
                    load("w2", 0, ffn2_done)
                    load("b2", 0, y_added)
                    load("w2", 1, ffn2_done)
                    load("b2", 1, y_added)
                if t is not None:
                    sp.wait_ge(slots_ready, t + 1)
                    sp.dma_start(slots_dram.rearrange("w p s -> p w s"), slots[:, :, :]).then_inc(slots_stored, 16)
                    sp.wait_ge(slots_stored, 16 * (t + 1))
                    sp.dma_start(slot_rows[:, :], slots_dram.rearrange("w (e g) s -> (w e) (g s)", g=G)) \
                        .then_inc(slots_loaded, 16)

            steps(sp, step)
            sp.wait_ge(scattered[1], NF * 48)

        @block.gpsimd
        def _(pool):
            pool.memset(ident[:, :], 0.0).then_inc(pool_setup, 1)
            pool.iota(slot_base_i[:, :], pattern=[[0, 1]], base=0, channel_multiplier=1).then_inc(pool_setup, 1)
            pool.wait_ge(pool_setup, 2)
            pool.affine_select(out=ident[:, :], in_=ident[:, :], compare_op=ALU.not_equal, fill=1.0, base=0,
                               pattern=[[-1, P]], channel_multiplier=1).then_inc(pool_setup, 1)
            pool.iota(dist_bias[:, :, :], pattern=[[-P, TILES], [1, SP]], base=0, channel_multiplier=-1,
                      allow_small_or_imprecise_dtypes=True).then_inc(pool_setup, 1)
            pool.wait_ge(pool_setup, 4)
            pool.tensor_scalar(dist_bias[:, :, :], dist_bias[:, :, :], SLOPE, None, ALU.mult).then_inc(pool_setup, 1)
            pool.wait_ge(pool_setup, 5)
            pool.affine_select(out=dist_bias[:, :, :], in_=dist_bias[:, :, :], compare_op=ALU.is_ge, fill=NEG, base=0,
                               pattern=[[P, TILES], [-1, SP]], channel_multiplier=1).then_inc(pool_setup, 1)
            pool.wait_ge(pool_setup, 6)

            def gathers(f, g):
                for half in range(2):
                    pool.wait_ge(gather_idx_ready, f + 1)
                    if not (isinstance(f, int) and f == 0):
                        pool.wait_ge(xg_transposed, f * 2 - 1 + half)
                    alone(pool)
                    for tt in range(TILES):
                        n = ROWS[tt]
                        pool.indirect_dma_start(
                            out=xg[half][0:n, tt, :], out_offset=None, in_=xn2_rows[g],
                            in_offset=bass.IndirectOffsetOnAxis(ap=gather_idx[0:n, tt, half:half + 1], axis=0)) \
                            .then_inc(gathered[half], 16)

            def scatters(f):
                for half in range(2):
                    pool.wait_ge(y_ready, f * 2 + half + 1)
                    pool.wait_ge(table_ready, f + 1)
                    if half:
                        pool.wait_ge(scattered[0], f * 48 + 48)
                    elif not (isinstance(f, int) and f == 0):
                        pool.wait_ge(scattered[1], f * 48)
                    alone(pool)
                    for tt in range(TILES):
                        n = ROWS[tt]
                        pool.indirect_dma_start(
                            out=out_rows,
                            out_offset=bass.IndirectOffsetOnAxis(ap=scatter_idx[0:n, tt, half:half + 1], axis=0),
                            in_=y[half][0:n, tt, :], in_offset=None, compute_op=ALU.add) \
                            .then_inc(scattered[half], 16)

            def step(xb, yb, rb, k, rg, t, f, fk, fg, dj, prep):
                if f is not None and (not prep or t is not None):
                    scatters(f)
                if prep:
                    if t is not None:
                        pool.wait_ge(rows_stored, 64 * G * (t + 1))
                    gathers(0 if f is None else f + 1, fg if t is None else t)
                if f is not None and not (not prep or t is not None):
                    scatters(f)

            steps(pool, step)
            pool.wait_ge(scattered[0], NF * 48)
            pool.wait_ge(scattered[1], NF * 48)

        @block.tensor
        def _(pe):
            mm, tr = nc.tensor.matmul, nc.tensor.transpose
            pe.wait_ge(pool_setup, 6)
            pe.wait_ge(consts_loaded, 16 * 7)
            pe.wait_ge(vec_setup, 2)
            for c in range(CTX):
                tr(ps[5][:, c * P:(c + 1) * P], w_tok_raw[:, c * P:(c + 1) * P], ident[:, :])
            tr(ps[6][:, 0:P], w_v_raw[:, :], ident[:, :])
            tr(ps[6][:, P:P + E], b1_raw[:, :], ident[0:E, 0:E]).then_inc(weights_transposed, 1)
            pe.wait_ge(weights_ready, 1)

            def step(xb, yb, rb, k, rg, t, f, fk, fg, dj, prep):
                def first(i):
                    return isinstance(i, int) and i == 0

                def gather_transpose(half):
                    pe.wait_ge(gathered[half], f * 48 + 48)
                    if not (first(f) and half == 0):
                        pe.wait_ge(xgT_copied, f * 2 + half)
                    for tt in range(TILES):
                        n = ROWS[tt]
                        last = tr(ps_g[:, tt * P:tt * P + n], xg[half][0:n, tt, :], ident[0:n, 0:n])
                    last.then_inc(xg_transposed, 1)

                def ffn1(half):
                    pe.wait_ge(xgT_copied, f * 2 + half + 1)
                    pe.wait_ge(w1_loaded[half], f * 16 + 16)
                    if not (first(f) and half == 0):
                        pe.wait_ge(u_copied, f * 2 + half)
                    mm(ps_u[:, 0:SLOTS], w1_sb[half][:, :], xgT[:, :], start=True, stop=True).then_inc(ffn1_done, 1)

                def ffn2(half):
                    pe.wait_ge(hid_ready, f * 2 + half + 1)
                    pe.wait_ge(w2_loaded[half], f * 16 + 16)
                    if not (first(f) and half == 0):
                        pe.wait_ge(y_added, f * 2 + half)
                    for tt in range(TILES):
                        n = ROWS[tt]
                        last = mm(ps_y[0:n, tt * P:(tt + 1) * P], hidT[:, tt * P:tt * P + n], w2_sb[half][:, :],
                                  start=True, stop=True)
                    last.then_inc(ffn2_done, 1)

                if f is not None:
                    gather_transpose(0)
                if yb is not None:
                    pe.wait_ge(xn_ready, yb + 1)
                    if not first(yb):
                        pe.wait_ge(q_copied, yb)
                    for tt in range(TILES):
                        last = tr(ps_q[:, tt * P:(tt + 1) * P], xn[:, tt, :], ident[:, :])
                    last.then_inc(xn_transposed, 1)
                if f is not None:
                    ffn1(0)
                if yb is not None:
                    pe.wait_ge(xnT_copied, yb + 1)
                    mm(ps_q[:, 0:SP], w_qk_sb[:, :], xnT[:, :], start=True, stop=True).then_inc(q_done, 1)
                if f is not None:
                    gather_transpose(1)
                if rb is not None:
                    pe.wait_ge(xn2_ready, rb + 1)
                    for tt in range(TILES):
                        last = tr(ps_v[:, tt * P:(tt + 1) * P], xn2[:, tt, :], ident[:, :])
                    last.then_inc(xn2_transposed, 1)
                if yb is not None:
                    pe.wait_ge(q_copied, yb + 1)
                    if not first(yb):
                        pe.wait_ge(pT_copied, yb * 2)
                    for tt in range(TILES):
                        bank, off = (ps_s[0], SO[tt]) if tt < 2 else (ps_s[1], 0)
                        last = mm(bank[:, off:off + SW[tt]], qT[:, tt * P:(tt + 1) * P], xnT[:, 0:SW[tt]],
                                  start=True, stop=True)
                        if tt > 0:
                            last.then_inc(s_done, 1)
                if xb is not None:
                    pe.wait_ge(x_loaded, xb * 32 + 32)
                    if not first(xb):
                        pe.wait_ge(conv_added, xb)
                    for tt in range(TILES):
                        n = P if tt < TILES - 1 else LASTX
                        last = tr(ps_x[:, tt * P:tt * P + n], xs[0:n, tt, :], ident[0:n, 0:n])
                    last.then_inc(x_transposed, 1)
                if rb is not None:
                    pe.wait_ge(xn2T_copied, rb + 1)
                    for tt in range(TILES):
                        last = mm(ps_v[:, SP + tt * E:SP + (tt + 1) * E], xn2T[:, tt * P:(tt + 1) * P],
                                  w_gate_sb[:, :], start=True, stop=True)
                    last.then_inc(logits_done, 1)
                if f is not None:
                    ffn1(1)
                if xb is not None:
                    pe.wait_ge(xT_copied, xb + 1)
                    for tt in range(TILES):
                        for c in range(CTX):
                            last = mm(ps_x[:, tt * P:(tt + 1) * P], xT[:, tt * P + c:tt * P + c + P],
                                      w_tokT[:, c * D:(c + 1) * D], start=(c == 0), stop=(c == CTX - 1))
                    last.then_inc(conv_done, 1)
                if yb is not None:
                    if rb is not None:
                        pe.wait_ge(logits_read, rb + 1)
                    for tt in range(TILES):
                        last = mm(ps_v[:, tt * P:(tt + 1) * P], xnT[:, tt * P:(tt + 1) * P], w_vT[:, :],
                                  start=True, stop=True)
                    last.then_inc(v_done, 1)
                if t is not None:
                    pe.wait_ge(aff_ready, G * (t + 1))
                    if f is not None:
                        pe.wait_ge(y_added, f * 2)
                    for tt in range(TILES):
                        n = P if tt < TILES - 1 else LAST
                        last = tr(ps_y[:, tt * P:tt * P + n], aff[0:n, tt, :, :].rearrange("p e g -> p (e g)"),
                                  ident[0:n, 0:n])
                    last.then_inc(aff_transposed, 1)
                if f is not None:
                    if t is not None:
                        pe.wait_ge(t_vec, 18 * t + 1)
                    ffn2(0)
                if yb is not None:
                    pe.wait_ge(exp_done, yb * 3 + 3)
                    for tt in range(TILES):
                        bank, off = (ps_s[0], SO[tt]) if tt < 2 else (ps_s[1], 0)
                        for c in range(tt + 1):
                            last = tr(bank[:, off + c * P:off + (c + 1) * P],
                                      probs[:, SO[tt] + c * P:SO[tt] + (c + 1) * P], ident[:, :])
                        if tt > 0:
                            last.then_inc(pT_done, 1)
                if f is not None:
                    ffn2(1)
                if yb is not None:
                    pe.wait_ge(v_added, yb + 1)
                    pe.wait_ge(pT_copied, yb * 2 + 2)
                    for tt in range(TILES):
                        for c in range(tt + 1):
                            last = mm(ps_v[:, tt * P:(tt + 1) * P], probsT[:, SO[tt] // P + c, :], v[:, c, :],
                                      start=(c == 0), stop=(c == tt))
                    last.then_inc(pv_done, 1)
                if t is not None:
                    pe.wait_ge(slots_loaded, 16 * (t + 1))
                    if f is not None:
                        pe.wait_ge(y_added, f * 2 + 2)
                    for tt in range(TILES):
                        n = ROWS[tt]
                        last = tr(ps_y[0:n, tt * 2 * E:(tt + 1) * 2 * E], slot_rows[:, tt * P:tt * P + n],
                                  ident[0:2 * E, 0:2 * E])
                    last.then_inc(tab_transposed, 1)

            steps(pe, step)

        @block.scalar
        def _(act):
            A = nc.scalar.activation
            act.wait_ge(weights_transposed, 1)
            A(w_tokT[:, :], ps[5][:, 0:CTX * D], ACT.Copy)
            A(w_vT[:, :], ps[6][:, 0:P], ACT.Copy)
            A(b1T[:, :], ps[6][:, P:P + E], ACT.Copy).then_inc(weights_ready, 1)

            def step(xb, yb, rb, k, rg, t, f, fk, fg, dj, prep):
                def first(i):
                    return isinstance(i, int) and i == 0

                def copy_gathered(half):
                    act.wait_ge(xg_transposed, f * 2 + half + 1)
                    A(xgT[:, :], ps_g[:, 0:SLOTS], ACT.Copy, scale=0.5).then_inc(xgT_copied, 1)

                def bias_and_square(half):
                    act.wait_ge(ffn1_done, f * 2 + half + 1)
                    if half == 0:
                        act.wait_ge(pair_ready, f + 1)
                    if not (first(f) and half == 0):
                        act.wait_ge(hid_ready, f * 2 + half)
                    A(u[:, :], ps_u[:, 0:SLOTS], ACT.Identity, bias=half_b1[:, half:half + 1]).then_inc(u_copied, 1)
                    act.wait_ge(u_copied, f * 2 + half + 1)
                    A(u_sq[:, :], u[:, :], ACT.Square, scale=2.0 * GELU_C ** 0.5).then_inc(u_squared, 1)

                def tanh(half):
                    act.wait_ge(gelu_in_ready, f * 2 + half + 1)
                    A(tanh_out[:, :], gelu_in[:, :], ACT.Tanh, scale=2.0 * GELU_S).then_inc(tanh_done, 1)

                def weigh(half):
                    act.wait_ge(y_added, f * 2 + half + 1)
                    for tt in range(TILES):
                        last = A(y[half][:, tt, :], y[half][:, tt, :], ACT.Copy, scale=gate[:, tt, half:half + 1])
                    last.then_inc(y_ready, 1)

                if f is not None:
                    copy_gathered(0)
                if yb is not None:
                    act.wait_ge(xn_transposed, yb + 1)
                    A(xnT[:, :], ps_q[:, 0:SP], ACT.Copy).then_inc(xnT_copied, 1)
                if f is not None:
                    bias_and_square(0)
                if yb is not None:
                    act.wait_ge(q_done, yb + 1)
                    A(qT[:, :], ps_q[:, 0:SP], ACT.Copy, scale=SCALE).then_inc(q_copied, 1)
                if f is not None:
                    copy_gathered(1)
                if rb is not None:
                    act.wait_ge(xn2_transposed, rb + 1)
                    A(xn2T[:, :], ps_v[:, 0:SP], ACT.Copy).then_inc(xn2T_copied, 1)
                if f is not None:
                    tanh(0)
                if xb is not None:
                    act.wait_ge(x_transposed, xb + 1)
                    A(xT[:, 0:NTOK], ps_x[:, 0:NTOK], ACT.Copy).then_inc(xT_copied, 1)
                if rb is not None:
                    act.wait_ge(logits_read, rb + 1)
                    A(r_exp[:, :, :], r_exp[:, :, :], ACT.Exp).then_inc(r_exp_done, 1)
                if yb is not None:
                    act.wait_ge(max_ready, yb + 1)
                    for tt in range(TILES):
                        tile = probs[:, SO[tt]:SO[tt] + SW[tt]]
                        A(tile, tile, ACT.Exp, bias=neg_max[:, tt:tt + 1],
                          accum_out=row_sum[:, tt:tt + 1]).then_inc(exp_done, 1)
                if f is not None:
                    bias_and_square(1)
                if f is not None:
                    tanh(1)
                if yb is not None:
                    for i in range(2):
                        act.wait_ge(pT_done, yb * 2 + i + 1)
                        A(probsT[:, 3 * i:3 * i + 3, :].rearrange("p a b -> p (a b)"), ps_s[i][:, 0:SP],
                          ACT.Copy).then_inc(pT_copied, 1)
                if xb is not None:
                    act.wait_ge(conv_added, xb + 1)
                    A(h[:, :, :], hpre[:, :, :], ACT.Relu).then_inc(relu_done, 1)
                if f is not None:
                    weigh(0)
                    weigh(1)

            steps(act, step)

        @block.vector
        def _(dve):
            V = nc.vector
            V.memset(xT[:, NTOK:XCOLS], 0.0).then_inc(vec_setup, 1)
            V.memset(ps_y[:, :], 0.0).then_inc(vec_setup, 1)
            dve.wait_ge(pool_setup, 6)
            V.tensor_scalar(slot_base_i[:, :], slot_base_i[:, :], G - 1, None, ALU.bitwise_and).then_inc(vec_setup, 1)
            dve.wait_ge(vec_setup, 3)
            V.tensor_scalar(slot_base[:, :], slot_base_i[:, :], float(S), None, ALU.mult).then_inc(vec_setup, 1)
            dve.wait_ge(vec_setup, 4)
            dve.wait_ge(weights_ready, 1)

            def chain(sem_, base):
                count = [0]

                def add(ins):
                    count[0] += 1
                    ins.then_inc(sem_, 1)

                def link(ins, single=False):
                    add(ins)
                    dve.wait_ge(sem_, base + count[0])
                    if single:
                        alone(dve)
                return link, add

            def layer_norm(link, src, dst, s):
                for tt in range(TILES):
                    V.bn_stats(s["stats"][:, tt, :], src[:, tt, :]) if tt < TILES - 1 else \
                        link(V.bn_stats(s["stats"][:, tt, :], src[:, tt, :]), single=True)
                for tt in range(TILES):
                    V.bn_aggr(s["mv"][:, tt, :], s["stats"][:, tt, :]) if tt < TILES - 1 else \
                        link(V.bn_aggr(s["mv"][:, tt, :], s["stats"][:, tt, :]))
                var, yy, t = (s[n][:, :, 0] for n in ("var", "y", "t"))
                link(V.tensor_scalar(var, s["mv"][:, :, 1], EPS, None, ALU.add))
                link(V.tensor_scalar(yy.bitcast(I32), var.bitcast(I32), 1, None, ALU.logical_shift_right))
                link(V.tensor_scalar(yy.bitcast(I32), yy.bitcast(I32), -1.0, RSQRT_MAGIC, ALU.mult, ALU.add))
                for _ in range(3):
                    link(V.scalar_tensor_tensor(t, yy, -0.5, yy, ALU.mult, ALU.mult))
                    link(V.tensor_tensor(t, t, var, ALU.mult))
                    link(V.scalar_tensor_tensor(yy, t, 1.5, yy, ALU.add, ALU.mult))
                for tt in range(TILES):
                    last = V.tensor_scalar(dst[:, tt, :], src[:, tt, :], s["mv"][:, tt, 0:1], s["y"][:, tt, 0:1],
                                           ALU.subtract, ALU.mult)
                return last

            def step(xb, yb, rb, k, rg, t, f, fk, fg, dj, prep):
                def first(i):
                    return isinstance(i, int) and i == 0

                def scatter_table():
                    if not first(f):
                        dve.wait_ge(scattered[1], f * 48)
                        dve.wait_ge(y_ready, f * 2)
                        alone(dve)
                    e = (dj + fk) * 2
                    V.tensor_copy(gate[:, :, :], tab_gate[:, :, bass.ds(e, 2)])
                    V.tensor_scalar(scatter_idx[:, :, :], tab_idx[:, :, bass.ds(e, 2)], float(fg * G * S), None,
                                    ALU.add).then_inc(table_ready, 1)

                def next_indices():
                    nf = 0 if f is None else f + 1
                    if f is not None:
                        dve.wait_ge(gathered[0], f * 48 + 48)
                        dve.wait_ge(gathered[1], f * 48 + 48)
                        alone(dve)
                    e = (dj + ((fk + 1) % PAIRS if f is not None else 0)) * 2
                    V.tensor_copy(gather_idx[:, :, :], tab_idx[:, :, bass.ds(e, 2)]).then_inc(gather_idx_ready, 1)

                def gelu_in_(half):
                    dve.wait_ge(u_squared, f * 2 + half + 1)
                    V.scalar_tensor_tensor(gelu_in[:, :], u_sq[:, :], 1.0, u[:, :], ALU.add, ALU.mult) \
                        .then_inc(gelu_in_ready, 1)

                def hidden(half):
                    dve.wait_ge(tanh_done, f * 2 + half + 1)
                    if not (first(f) and half == 0):
                        dve.wait_ge(ffn2_done, f * 2 + half)
                    V.scalar_tensor_tensor(hidT[:, :], tanh_out[:, :], 1.0, u[:, :], ALU.add, ALU.mult) \
                        .then_inc(hid_ready, 1)

                def add_b2(half):
                    dve.wait_ge(ffn2_done, f * 2 + half + 1)
                    dve.wait_ge(b2_loaded[half], f * 16 + 16)
                    if not first(f):
                        dve.wait_ge(scattered[half], f * 48)
                    V.tensor_tensor(y[half][:, :, :], ps_y[:, 0:SP].rearrange("p (a b) -> p a b", a=TILES),
                                    b2_rep[half][:, :].unsqueeze(1).to_broadcast([P, TILES, D]), ALU.add) \
                        .then_inc(y_added, 1)

                ylink, yadd = chain(y_vec, None if yb is None else yb * 18)
                rlink, radd = chain(r_vec, None if rb is None else rb * 3)
                if f is not None:
                    V.tensor_scalar(half_b1[:, :], b1T[:, bass.ds((dj + fk) * 2, 2)], 0.5, None, ALU.mult) \
                        .then_inc(pair_ready, 1)
                    if prep and t is None:
                        next_indices()
                if yb is not None:
                    ylink(V.tensor_copy(hres[:, :, :], h[:, :, :]))
                if f is not None:
                    gelu_in_(0)
                if yb is not None:
                    for tt in range(TILES):
                        bank, off = (ps_s[0], SO[tt]) if tt < 2 else (ps_s[1], 0)
                        dve.wait_ge(s_done, yb * 2 + 1 + (tt == 2))
                        alone(dve)
                        last = V.tensor_tensor_reduce(
                            out=probs[:, SO[tt]:SO[tt] + SW[tt]], in0=bank[:, off:off + SW[tt]],
                            in1=dist_bias[:, tt, 0:SW[tt]], scale=1.0, scalar=NEG, op0=ALU.add, op1=ALU.max,
                            accum_out=row_max[:, tt:tt + 1])
                    ylink(last)
                    V.tensor_scalar(neg_max[:, :], row_max[:, :], -1.0, None, ALU.mult).then_inc(max_ready, 1)
                if rb is not None:
                    logits = ps_v[:, SP:SP + TILES * E].rearrange("p (a e) -> p a e", a=TILES)
                    dve.wait_ge(logits_done, rb + 1)
                    rlink(V.tensor_reduce(r_max[:, :, 0], logits, AX_X, ALU.max))
                    V.tensor_tensor(r_exp[:, :, :], logits, r_max[:, :, :].to_broadcast([P, TILES, E]),
                                    ALU.subtract).then_inc(logits_read, 1)
                if f is not None:
                    hidden(0)
                if rb is not None:
                    dve.wait_ge(r_exp_done, rb + 1)
                    rlink(V.tensor_reduce(r_sum[:, :, 0], r_exp[:, :, :], AX_X, ALU.add))
                    rlink(V.reciprocal(r_sum[:, :, :], r_sum[:, :, :]))
                    V.tensor_tensor(aff[:, :, :, bass.ds(dj + k, 1)].rearrange("p a e g -> p a (e g)"), r_exp[:, :, :],
                                    r_sum[:, :, :].to_broadcast([P, TILES, E]), ALU.mult).then_inc(aff_ready, 1)
                if f is not None:
                    gelu_in_(1)
                if xb is not None:
                    dve.wait_ge(conv_done, xb + 1)
                    if not first(xb):
                        dve.wait_ge(relu_done, xb)
                    V.tensor_tensor(hpre[:, :, :], ps_x[:, 0:SP].rearrange("p (a b) -> p a b", a=TILES),
                                    b_tok_rep[:, :].unsqueeze(1).to_broadcast([P, TILES, D]), ALU.add) \
                        .then_inc(conv_added, 1)
                if yb is not None:
                    dve.wait_ge(v_done, yb + 1)
                    V.tensor_tensor(v[:, :, :], ps_v[:, 0:SP].rearrange("p (a b) -> p a b", a=TILES),
                                    b_v_rep[:, :].unsqueeze(1).to_broadcast([P, TILES, D]), ALU.add) \
                        .then_inc(v_added, 1)
                if t is not None:
                    tlink, tadd = chain(t_vec, t * 18)
                    dve.wait_ge(aff_transposed, t + 1)
                    tlink(V.tensor_copy(affT[:, :], ps_y[:, 0:S]))
                    for r in range(ROUNDS):
                        top = top_val[:, 8 * r:8 * r + 8]
                        tlink(V.max(top, affT[:, :]))
                        place = V.max_index(top_idx[:, 8 * r:8 * r + 8], top, affT[:, :])
                        if r < ROUNDS - 1:
                            tadd(place)
                            tlink(V.match_replace(affT[:, :], top, affT[:, :], -1.0))
                        else:
                            tlink(place)
                    if t > 0:
                        dve.wait_ge(slots_stored, 16 * t)
                    V.tensor_scalar(slots[:, 0, :], top_idx[:, 0:CAP], slot_base[:, 0:1], None, ALU.add)
                    V.tensor_copy(slots[:, 1, :], top_val[:, 0:CAP]).then_inc(slots_ready, 1)
                if f is not None:
                    hidden(1)
                if f is not None:
                    scatter_table()
                    add_b2(0)
                if xb is not None:
                    dve.wait_ge(relu_done, xb + 1)
                    xlink, xadd = chain(x_vec, xb * 14)
                    if not first(xb):
                        dve.wait_ge(xn_transposed, xb)
                        alone(dve)
                    layer_norm(xlink, h, xn, ln[0]).then_inc(xn_ready, 1)
                if f is not None:
                    add_b2(1)
                if yb is not None:
                    dve.wait_ge(exp_done, yb * 3 + 3)
                    ylink(V.reciprocal(row_inv[:, :], row_sum[:, :]))
                    dve.wait_ge(pv_done, yb + 1)
                    if not first(yb):
                        dve.wait_ge(rows_stored, yb * 64)
                        dve.wait_ge(xn2_transposed, yb)
                    for tt in range(TILES):
                        last = V.scalar_tensor_tensor(h2[:, tt, :], ps_v[:, tt * P:(tt + 1) * P],
                                                      row_inv[:, tt:tt + 1], hres[:, tt, :], ALU.mult, ALU.add)
                    ylink(last, single=True)
                    layer_norm(ylink, h2, xn2, ln[1]).then_inc(xn2_ready, 1)
                if t is not None:
                    dve.wait_ge(tab_transposed, t + 1)
                    tab = ps_y[:, 0:TILES * 2 * E].rearrange("p (a w e) -> p a w e", a=TILES, w=2)
                    V.tensor_copy(tab_idx[:, :, :], tab[:, :, 0, :])
                    V.tensor_copy(tab_gate[:, :, :], tab[:, :, 1, :]).then_inc(tab_ready, 1)
                    dve.wait_ge(tab_ready, t + 1)
                    next_indices()

            steps(dve, step)


_INS = ["x", "L0_tok_weight", "L0_tok_bias", "L0_attn_W_qk", "L0_attn_W_v", "L0_attn_b_v", "L0_ffn_gate_weight",
        "L0_ffn_w1", "L0_ffn_b1", "L0_ffn_w2", "L0_ffn_b2"]


def kernel(**inputs):
    import numpy as _np
    import concourse.bacc as _bacc
    from concourse import mybir as _mybir
    from concourse.bass_utils import run_bass_kernel_spmd as _run

    nc = _bacc.Bacc("TRN2", target_bir_lowering=False, num_devices=1)
    arrays, args = {}, []
    for name in _INS:
        a = _np.ascontiguousarray(inputs[name])
        arrays[f"in_{name}"] = a
        args.append(nc.dram_tensor(f"in_{name}", a.shape, _mybir.dt.from_np(a.dtype), kind="ExternalInput").ap())
    batch, tokens, d = inputs["x"].shape
    rows = tokens - inputs["L0_tok_weight"].shape[1] // d + 1
    experts = inputs["L0_ffn_gate_weight"].shape[1]
    f32 = _mybir.dt.float32
    out = nc.dram_tensor("out_0", (batch, rows, d), f32, kind="ExternalOutput").ap()
    group = 128 // experts
    xn2_rows = [nc.dram_tensor(f"xn2_rows_{i}", (group * rows, d), f32).ap() for i in range(batch // group)]
    slots_dram = nc.dram_tensor("slots_scratch", (2, 128, rows // experts * 2), f32).ap()
    audio_tower_block(nc, *args, out, xn2_rows, slots_dram)
    r = _run(nc, [arrays], core_ids=[0])
    return r.results[0]["out_0"]
```

```python
from contextlib import ExitStack

import concourse.bass as bass
from concourse import mybir

F32 = mybir.dt.float32
BF16 = mybir.dt.bfloat16
I32 = mybir.dt.int32
U32 = mybir.dt.uint32
ALU = mybir.AluOpType
ACT = mybir.ActivationFunctionType
AX_X = mybir.AxisListType.X

P = 128
NEG = -3.0e38


class Step:

    def __init__(self, j, x, a, c, r, r_in_group, r_group, t, tables, f, f_group, expert, next_expert, next_group,
                 prepares):
        self.j, self.x, self.a, self.c, self.r, self.f = j, x, a, c, r, f
        self.t, self.tables = t, tables
        self.r_in_group, self.r_group, self.f_group = r_in_group, r_group, f_group
        self.expert, self.next_expert, self.next_group, self.prepares = expert, next_expert, next_group, prepares


def first(i):
    return isinstance(i, int) and i == 0


def audio_tower_block(nc, x, w_tok, b_tok, w_qk, w_v, b_v, w_gate, w1, b1, w2, b2, out, xn2_rows, slots_dram):
    B, NTOK, D = x.shape
    CTX = w_tok.shape[1] // D
    S = NTOK - CTX + 1
    E = w_gate.shape[1]
    CAP = S // E * 2
    TILES = -(-S // P)
    SP = TILES * P
    LAST = S - (TILES - 1) * P
    LASTX = NTOK - (TILES - 1) * P
    G = P // E
    GROUPS = B // G
    SLOTS = G * CAP
    ROUNDS = -(-CAP // 8)
    LAST_SLOTS = SLOTS - 2 * P
    PAIRS = E // 2
    NF = GROUPS * PAIRS
    SCALE = float(D) ** -0.5
    EPS = 1e-5
    SLOPE = 0.5
    GELU_C = 0.044715
    GELU_S = 0.7978845608028654
    RSQRT_MAGIC = 1597463007.0 + 0.5 * (2.0 ** 31 - 2.0 ** 23)
    assert TILES == 3 and D == P and G * E == P and SLOTS <= 3 * P and G == PAIRS
    XCOLS = (TILES - 1) * P + P + CTX - 1
    ROWS = [P, P, LAST_SLOTS]
    SW = [P * (t + 1) for t in range(TILES)]
    SO = [0, P, 3 * P]

    out_rows = out.rearrange("b s d -> (b s) d")
    x_rows = x.rearrange("b s d -> (b s) d")

    with ExitStack() as ctx:
        def sb(name, shape, dt=F32):
            return ctx.enter_context(nc.sbuf_tensor(name, shape, dt))

        def sem(name):
            return ctx.enter_context(nc.semaphore(name))

        ident = sb("ident", [P, P])
        dist_bias = sb("dist_bias", [P, TILES, SP])
        w_tok_raw = sb("w_tok_raw", [P, CTX * D])
        w_v_raw = sb("w_v_raw", [P, D])
        b1_raw = sb("b1_raw", [E, D])
        w_tokT = sb("w_tokT", [P, CTX * D])
        w_vT = sb("w_vT", [P, D])
        b1T = sb("b1T", [P, E])
        w_qk_sb = sb("w_qk_sb", [P, D])
        w_gate_sb = sb("w_gate_sb", [P, E])
        bias_raw = sb("bias_raw", [96, (2 + E) * D])
        bias_parts = sb("bias_parts", [96, 2, (2 + E) * D], BF16)
        bias_rows = sb("bias_rows", [96, (2 + E) * D], BF16)
        ones_bf = sb("ones_bf", [96, P], BF16)
        slot_base = sb("slot_base", [P, 1])
        slot_base_i = sb("slot_base_i", [P, 1], I32)
        xs = sb("xs", [P, TILES, D])
        xT = sb("xT", [P, XCOLS])
        h = sb("h", [P, TILES, D])
        xn = sb("xn", [P, TILES, D])
        hres = sb("hres", [P, TILES, D])
        hnext = sb("hnext", [P, TILES, D])
        xnT = sb("xnT", [P, SP])
        qT = sb("qT", [P, SP])
        v = sb("v", [P, TILES, D])
        probs = sb("probs", [P, 6 * P])
        row_max = sb("row_max", [P, TILES])
        neg_max = sb("neg_max", [P, TILES])
        row_sum = sb("row_sum", [P, TILES])
        row_inv = sb("row_inv", [P, TILES])
        probsT = sb("probsT", [P, 6, P])
        h2 = sb("h2", [P, TILES, D])
        xn2 = sb("xn2", [P, TILES, D])
        stats = sb("stats", [P, 2, TILES, 6])
        mv = sb("mv", [P, 2 * TILES, 2])
        nv = sb("nv", [P, 2 * TILES])
        rstd = sb("rstd", [P, 2 * TILES])
        sq = sb("sq", [P, 2 * TILES])
        xn2T = sb("xn2T", [P, SP])
        r_max = sb("r_max", [P, TILES, 1])
        r_exp = sb("r_exp", [P, TILES, E])
        r_sum = sb("r_sum", [P, TILES, 1])
        aff = sb("aff", [P, TILES, E, G])
        affT = sb("affT", [P, S])
        top_val = sb("top_val", [P, 8 * ROUNDS])
        top_idx = sb("top_idx", [P, 8 * ROUNDS], U32)
        slots = sb("slots", [P, 2, CAP])
        slot_rows = sb("slot_rows", [2 * E, SLOTS])
        tab_idx = sb("tab_idx", [P, TILES, E], I32)
        tab_gate = sb("tab_gate", [P, TILES, E])
        gather_idx = sb("gather_idx", [P, 2, TILES], I32)
        scatter_idx = sb("scatter_idx", [P, TILES, 2], I32)
        gate = sb("gate", [P, TILES, 2])
        half_b1 = sb("half_b1", [P, 2])
        w1_sb = [sb(f"w1_{i}", [P, D]) for i in "ab"]
        w2_sb = [sb(f"w2_{i}", [P, D]) for i in "ab"]
        xg = [sb(f"xg_{i}", [P, TILES, D]) for i in "ab"]
        y = [sb(f"y_{i}", [P, TILES, D]) for i in "ab"]
        xgT = [sb(f"xgT_{i}", [P, SLOTS]) for i in "ab"]
        u = [sb(f"u_{i}", [P, SLOTS]) for i in "ab"]
        u_sq = [sb(f"u_sq_{i}", [P, SLOTS]) for i in "ab"]
        gelu_in = [sb(f"gelu_in_{i}", [P, SLOTS]) for i in "ab"]
        tanh_out = [sb(f"tanh_out_{i}", [P, SLOTS]) for i in "ab"]
        hidT = [sb(f"hidT_{i}", [P, SLOTS]) for i in "ab"]

        ps = [ctx.enter_context(nc.psum_tensor(f"bank{i}", [P, 512], F32)) for i in range(8)]
        ps_x = ps[1]
        ps_q = ps[0]
        ps_v = ps[2]
        ps_s = [ps[3], ps[4]]
        ps_f = [ps[5], ps[6]]
        ps_y = ps[7]

        consts_loaded = sem("consts_loaded")
        pool_setup = sem("pool_setup")
        vec_setup = sem("vec_setup")
        weights_transposed = sem("weights_transposed")
        weights_ready = sem("weights_ready")
        x_loaded = sem("x_loaded")
        x_transposed = sem("x_transposed")
        xT_copied = sem("xT_copied")
        conv_done = sem("conv_done")
        relu_done = sem("relu_done")
        x_vec = sem("x_vec")
        x_stats = sem("x_stats")
        h_kept = sem("h_kept")
        res_kept = sem("res_kept")
        v_copied = sem("v_copied")
        a_vec = sem("a_vec")
        c_vec = sem("c_vec")
        rsqrt_vec = sem("rsqrt_vec")
        bias_loaded = sem("bias_loaded")
        bias_ready = sem("bias_ready")
        b2_ready = sem("b2_ready")
        vec_split = sem("vec_split")
        pool_split = sem("pool_split")
        xn_ready = sem("xn_ready")
        xn_transposed = sem("xn_transposed")
        xnT_copied = sem("xnT_copied")
        q_done = sem("q_done")
        q_copied = sem("q_copied")
        v_done = sem("v_done")
        s_done = sem("s_done")
        max_ready = sem("max_ready")
        exp_done = sem("exp_done")
        pT_done = sem("pT_done")
        pT_copied = sem("pT_copied")
        pv_done = sem("pv_done")
        attn_added = sem("attn_added")
        xn2_ready = sem("xn2_ready")
        rows_stored = sem("rows_stored")
        xn2_transposed = sem("xn2_transposed")
        xn2T_copied = sem("xn2T_copied")
        logits_done = sem("logits_done")
        logits_read = sem("logits_read")
        r_exp_done = sem("r_exp_done")
        r_vec = sem("r_vec")
        aff_ready = sem("aff_ready")
        aff_transposed = sem("aff_transposed")
        t_vec = sem("t_vec")
        slots_ready = sem("slots_ready")
        slots_stored = sem("slots_stored")
        slots_loaded = sem("slots_loaded")
        tab_transposed = sem("tab_transposed")
        tab_ready = sem("tab_ready")
        gather_idx_ready = [sem(f"gather_idx_ready_{i}") for i in "ab"]
        pair_ready = sem("pair_ready")
        table_ready = sem("table_ready")
        gathered = [sem(f"gathered_{i}") for i in "ab"]
        scattered = [sem(f"scattered_{i}") for i in "ab"]
        w1_loaded = [sem(f"w1_loaded_{i}") for i in "ab"]
        w2_loaded = [sem(f"w2_loaded_{i}") for i in "ab"]
        xg_transposed = sem("xg_transposed")
        xgT_copied = sem("xgT_copied")
        ffn1_done = sem("ffn1_done")
        u_copied = sem("u_copied")
        u_squared = sem("u_squared")
        gelu_in_ready = sem("gelu_in_ready")
        tanh_done = sem("tanh_done")
        hid_ready = sem("hid_ready")
        ffn2_done = sem("ffn2_done")
        y_ready = sem("y_ready")

        spacer = [sem("spacer_pool"), sem("spacer_vec")]

        block = ctx.enter_context(nc.Block())

        def steps(eng, step):
            last = B + 3 + PAIRS

            def one(j, lo):
                step(Step(
                    j=j,
                    x=j if lo < B else None,
                    a=j - 1 if 1 <= lo <= B else None,
                    c=j - 2 if 2 <= lo <= B + 1 else None,
                    r=j - 3 if 3 <= lo <= B + 2 else None,
                    r_in_group=(lo - 3) % G + (j - lo),
                    r_group=(lo - 3) // G,
                    t=(lo - 10) // G if 10 <= lo <= B + 2 and (lo - 10) % G == 0 else None,
                    tables=(lo - 11) // G if 11 <= lo <= B + 3 and (lo - 11) % G == 0 else None,
                    f=j - 12 if lo >= 12 else None,
                    f_group=(lo - 12) // PAIRS,
                    expert=2 * ((lo - 12) % PAIRS + (j - lo)),
                    next_expert=2 * ((lo - 11) % PAIRS + (j - lo)),
                    next_group=(lo - 11) // PAIRS,
                    prepares=11 <= lo < last))

            for lo, hi in ((0, 1), (1, 2), (2, 3), (3, 10), (10, 11), (11, 12), (12, 13), (13, 18), (18, 19),
                           (19, 20), (20, 26), (26, 27), (27, 28), (28, 31), (31, 32), (32, 33), (33, 34),
                           (34, 35), (35, 36), (36, last), (last, last + 1)):
                if hi - lo == 1:
                    one(lo, lo)
                else:
                    with eng.Fori(lo, hi) as j:
                        one(j, lo)

        def split_bias(eng, cols, done, ready):
            raw, rows = bias_raw[:, cols], bias_rows[:, cols]
            p1, p2 = (bias_parts[:, k, cols] for k in range(2))
            eng.tensor_copy(p1, raw).then_inc(done, 1)
            eng.wait_ge(done, 1)
            eng.tensor_copy(rows[0:1, :], p1[0:1, :]).then_inc(done, 1)
            eng.wait_ge(done, 2)
            eng.tensor_tensor(raw, raw, p1, ALU.subtract).then_inc(done, 1)
            eng.wait_ge(done, 3)
            eng.tensor_copy(p2, raw).then_inc(done, 1)
            eng.wait_ge(done, 4)
            eng.tensor_copy(rows[32:33, :], p2[32:33, :]).then_inc(done, 1)
            eng.wait_ge(done, 5)
            eng.tensor_tensor(raw, raw, p2, ALU.subtract).then_inc(done, 1)
            eng.wait_ge(done, 6)
            eng.tensor_copy(rows[64:65, :], raw[64:65, :]).then_inc(ready, 1)

        def alone(eng):
            eng.sem_inc(spacer[0 if eng is nc.gpsimd else 1], 1)

        @block.sync
        def _(sp):
            def load_x(b):
                r = b * NTOK
                sp.dma_start(xs[:, 0:2, :], x_rows[bass.ds(r, 2 * P), :].rearrange("(t p) d -> p t d", p=P)) \
                    .then_inc(x_loaded, 16)
                sp.dma_start(xs[0:LASTX, 2, :], x_rows[bass.ds(r + 2 * P, LASTX), :]).then_inc(x_loaded, 16)

            def store_rows(b, in_group, g):
                for dst, r, src in ((out_rows, b * S, h2), (xn2_rows[g], in_group * S, xn2)):
                    sp.dma_start(dst[bass.ds(r, 2 * P), :].rearrange("(t p) d -> p t d", p=P), src[:, 0:2, :]) \
                        .then_inc(rows_stored, 16)
                    sp.dma_start(dst[bass.ds(r + 2 * P, LAST), :], src[0:LAST, 2, :]).then_inc(rows_stored, 16)

            def step(at):
                def load(weights, buf, loaded, half, used):
                    if at.f is not None:
                        sp.wait_ge(used, at.f * 2 + half + 1)
                    sp.dma_start(buf[half][:, :], weights[bass.ds(at.next_expert + half, 1)]
                                 .rearrange("a d n -> (a d) n")).then_inc(loaded[half], 16)

                if at.r is not None:
                    sp.wait_ge(xn2_ready, at.r + 1)
                    if not first(at.r):
                        sp.wait_ge(rows_stored, at.r * 64)
                    store_rows(at.r, at.r_in_group, at.r_group)
                if at.x is not None and not (isinstance(at.x, int) and at.x == B - 1):
                    sp.wait_ge(x_transposed, at.x + 1)
                    load_x(at.x + 1)
                if at.prepares:
                    load(w1, w1_sb, w1_loaded, 0, ffn1_done)
                    load(w1, w1_sb, w1_loaded, 1, ffn1_done)
                    load(w2, w2_sb, w2_loaded, 0, ffn2_done)
                    load(w2, w2_sb, w2_loaded, 1, ffn2_done)
                if at.t is not None:
                    sp.wait_ge(slots_ready, at.t + 1)
                    sp.dma_start(slots_dram.rearrange("w p s -> p w s"), slots[:, :, :]).then_inc(slots_stored, 16)
                    sp.wait_ge(slots_stored, 16 * (at.t + 1))
                    sp.dma_start(slot_rows[:, :], slots_dram.rearrange("w (e g) s -> (w e) (g s)", g=G)) \
                        .then_inc(slots_loaded, 16)

            load_x(0)
            for dst, src in ((w_tok_raw[:, :], w_tok), (w_v_raw[:, :], w_v), (b1_raw[:, :], b1),
                             (w_qk_sb[:, :], w_qk), (w_gate_sb[:, :], w_gate)):
                sp.dma_start(dst, src).then_inc(consts_loaded, 16)
            sp.wait_ge(vec_setup, 2)
            for part in range(3):
                row = bias_raw[32 * part:32 * part + 1, :]
                for col, src in ((0, b_tok.rearrange("(a d) -> a d", a=1)), (D, b_v.rearrange("(a d) -> a d", a=1)),
                                 (2 * D, b2.rearrange("(a e) d -> a (e d)", a=1))):
                    sp.dma_start(row[:, col:col + src.shape[1]], src).then_inc(bias_loaded, 16)
            steps(sp, step)
            sp.wait_ge(scattered[1], NF * 48)

        @block.gpsimd
        def _(pool):
            pool.memset(ident[:, :], 0.0).then_inc(pool_setup, 1)
            pool.iota(slot_base_i[:, :], pattern=[[0, 1]], base=0, channel_multiplier=1).then_inc(pool_setup, 1)
            pool.wait_ge(pool_setup, 2)
            pool.affine_select(out=ident[:, :], in_=ident[:, :], compare_op=ALU.not_equal, fill=1.0, base=0,
                               pattern=[[-1, P]], channel_multiplier=1).then_inc(pool_setup, 1)
            pool.iota(dist_bias[:, :, :], pattern=[[-P, TILES], [1, SP]], base=0, channel_multiplier=-1,
                      allow_small_or_imprecise_dtypes=True).then_inc(pool_setup, 1)
            pool.wait_ge(pool_setup, 4)
            pool.tensor_scalar(dist_bias[:, :, :], dist_bias[:, :, :], SLOPE, None, ALU.mult).then_inc(pool_setup, 1)
            pool.wait_ge(pool_setup, 5)
            pool.affine_select(out=dist_bias[:, :, :], in_=dist_bias[:, :, :], compare_op=ALU.is_ge, fill=NEG, base=0,
                               pattern=[[P, TILES], [-1, SP]], channel_multiplier=1).then_inc(pool_setup, 1)
            pool.wait_ge(pool_setup, 6)

            pool.wait_ge(bias_loaded, 16 * 9)
            split_bias(pool, slice(2 * D, (2 + E) * D), pool_split, b2_ready)
            pool.wait_ge(b2_ready, 1)

            def gather(f, half, g):
                pool.wait_ge(gather_idx_ready[half], f + 1)
                if not first(f):
                    pool.wait_ge(xg_transposed, f * 2 - 1 + half)
                alone(pool)
                for tt in range(TILES):
                    n = ROWS[tt]
                    pool.indirect_dma_start(
                        out=xg[half][0:n, tt, :], out_offset=None, in_=xn2_rows[g],
                        in_offset=bass.IndirectOffsetOnAxis(ap=gather_idx[0:n, half, tt:tt + 1], axis=0)) \
                        .then_inc(gathered[half], 16)

            def scatter(f, half):
                pool.wait_ge(y_ready, f * 2 + half + 1)
                pool.wait_ge(table_ready, f + 1)
                if half:
                    pool.wait_ge(scattered[0], f * 48 + 48)
                elif not first(f):
                    pool.wait_ge(scattered[1], f * 48)
                alone(pool)
                for tt in range(TILES):
                    n = ROWS[tt]
                    pool.indirect_dma_start(
                        out=out_rows,
                        out_offset=bass.IndirectOffsetOnAxis(ap=scatter_idx[0:n, tt, half:half + 1], axis=0),
                        in_=y[half][0:n, tt, :], in_offset=None, compute_op=ALU.add) \
                        .then_inc(scattered[half], 16)

            def step(at):
                if at.tables is not None:
                    pool.wait_ge(rows_stored, 64 * G * (at.tables + 1))
                if at.prepares:
                    gather(0 if at.f is None else at.f + 1, 0, at.next_group)
                if at.prepares:
                    gather(0 if at.f is None else at.f + 1, 1, at.next_group)
                if at.f is not None:
                    scatter(at.f, 0)
                if at.f is not None:
                    scatter(at.f, 1)

            steps(pool, step)
            pool.wait_ge(scattered[0], NF * 48)
            pool.wait_ge(scattered[1], NF * 48)

        @block.tensor
        def _(pe):
            mm, tr = nc.tensor.matmul, nc.tensor.transpose
            pe.wait_ge(pool_setup, 6)
            pe.wait_ge(consts_loaded, 16 * 5)
            pe.wait_ge(vec_setup, 5)
            for c in range(CTX):
                tr(ps[5][:, c * P:(c + 1) * P], w_tok_raw[:, c * P:(c + 1) * P], ident[:, :])
            tr(ps[6][:, 0:P], w_v_raw[:, :], ident[:, :])
            tr(ps[6][:, P:P + E], b1_raw[:, :], ident[0:E, 0:E]).then_inc(weights_transposed, 1)
            pe.wait_ge(weights_ready, 1)

            def bias(out_ap, col, start):
                return mm(out_ap, ones_bf[:, 0:out_ap.shape[0]], bias_rows[:, col], start=start, stop=False)

            def step(at):
                x, a, c, r, t, f = at.x, at.a, at.c, at.r, at.t, at.f

                def gather_transpose(half):
                    pe.wait_ge(gathered[half], f * 48 + 48)
                    if not first(f):
                        pe.wait_ge(u_copied, f * 2 + half - 1)
                    for tt in range(TILES):
                        n = ROWS[tt]
                        last = tr(ps_f[half][:, tt * P:tt * P + n], xg[half][0:n, tt, :], ident[0:n, 0:n])
                    last.then_inc(xg_transposed, 1)

                def ffn1(half):
                    pe.wait_ge(xgT_copied, f * 2 + half + 1)
                    pe.wait_ge(w1_loaded[half], f * 16 + 16)
                    mm(ps_f[half][:, 0:SLOTS], w1_sb[half][:, :], xgT[half][:, :], start=True, stop=True).then_inc(ffn1_done, 1)

                def ffn2(half):
                    pe.wait_ge(hid_ready, f * 2 + half + 1)
                    pe.wait_ge(w2_loaded[half], f * 16 + 16)
                    if not (first(f) and half == 0):
                        pe.wait_ge(y_ready, f * 2 + half)
                    for tt in range(TILES):
                        n = ROWS[tt]
                        tile = ps_y[0:n, tt * P:(tt + 1) * P]
                        bias(tile, bass.ds((at.expert + half + 2) * D, D), True)
                        last = mm(tile, hidT[half][:, tt * P:tt * P + n], w2_sb[half][:, :], start=False, stop=True)
                    last.then_inc(ffn2_done, 1)

                if x is not None:
                    pe.wait_ge(x_loaded, x * 32 + 32)
                    if not first(x):
                        pe.wait_ge(relu_done, x)
                    for tt in range(TILES):
                        n = P if tt < TILES - 1 else LASTX
                        last = tr(ps_x[:, tt * P:tt * P + n], xs[0:n, tt, :], ident[0:n, 0:n])
                    last.then_inc(x_transposed, 1)
                if f is not None:
                    gather_transpose(0)
                if f is not None:
                    gather_transpose(1)
                if x is not None:
                    pe.wait_ge(xT_copied, x + 1)
                    if first(x):
                        pe.wait_ge(bias_ready, 1)
                    for tt in range(TILES):
                        tile = ps_x[:, tt * P:(tt + 1) * P]
                        bias(tile, slice(0, D), True)
                        for k in range(CTX):
                            last = mm(tile, xT[:, tt * P + k:tt * P + k + P], w_tokT[:, k * D:(k + 1) * D],
                                      start=False, stop=(k == CTX - 1))
                    last.then_inc(conv_done, 1)
                if a is not None:
                    pe.wait_ge(xn_ready, a + 1)
                    if not first(a):
                        pe.wait_ge(q_copied, a)
                    for tt in range(TILES):
                        last = tr(ps_q[:, tt * P:(tt + 1) * P], xn[:, tt, :], ident[:, :])
                    last.then_inc(xn_transposed, 1)
                if c is not None:
                    pe.wait_ge(exp_done, c * 3 + 3)
                    if at.tables is not None:
                        pe.wait_ge(t_vec, 18 * at.tables + 1)
                    for tt in range(TILES):
                        bank, off = (ps_s[0], SO[tt]) if tt < 2 else (ps_s[1], 0)
                        for k in range(tt + 1):
                            last = tr(bank[:, off + k * P:off + (k + 1) * P],
                                      probs[:, SO[tt] + k * P:SO[tt] + (k + 1) * P], ident[:, :])
                        if tt > 0:
                            last.then_inc(pT_done, 1)
                if r is not None:
                    pe.wait_ge(xn2_ready, r + 1)
                    pe.wait_ge(attn_added, r + 1)
                    if c is not None:
                        pe.wait_ge(v_copied, c + 1)
                    for tt in range(TILES):
                        last = tr(ps_v[:, tt * P:(tt + 1) * P], xn2[:, tt, :], ident[:, :])
                    last.then_inc(xn2_transposed, 1)
                if f is not None:
                    ffn1(0)
                if r is not None:
                    pe.wait_ge(xn2T_copied, r + 1)
                    if not first(r):
                        pe.wait_ge(logits_read, r)
                    for tt in range(TILES):
                        last = mm(ps_v[:, SP + tt * E:SP + (tt + 1) * E], xn2T[:, tt * P:(tt + 1) * P],
                                  w_gate_sb[:, :], start=True, stop=True)
                    last.then_inc(logits_done, 1)
                if a is not None:
                    pe.wait_ge(xnT_copied, a + 1)
                    mm(ps_q[:, 0:SP], w_qk_sb[:, :], xnT[:, :], start=True, stop=True).then_inc(q_done, 1)
                if f is not None:
                    ffn1(1)
                if c is not None:
                    if r is not None:
                        pe.wait_ge(logits_read, r + 1)
                    pe.wait_ge(v_copied, c + 1)
                    pe.wait_ge(pT_copied, c * 2 + 2)
                    for tt in range(TILES):
                        for k in range(tt + 1):
                            last = mm(ps_v[:, tt * P:(tt + 1) * P], probsT[:, SO[tt] // P + k, :], v[:, k, :],
                                      start=(k == 0), stop=(k == tt))
                    last.then_inc(pv_done, 1)
                if at.tables is not None:
                    pe.wait_ge(slots_loaded, 16 * (at.tables + 1))
                    if f is not None and not first(f):
                        pe.wait_ge(y_ready, f * 2)
                    for tt in range(TILES):
                        n = ROWS[tt]
                        last = tr(ps_y[0:n, tt * 2 * E:(tt + 1) * 2 * E], slot_rows[:, tt * P:tt * P + n],
                                  ident[0:2 * E, 0:2 * E])
                    last.then_inc(tab_transposed, 1)
                if f is not None:
                    if at.tables is not None:
                        pe.wait_ge(tab_ready, at.tables + 1)
                    if first(f):
                        pe.wait_ge(b2_ready, 1)
                    ffn2(0)
                if a is not None:
                    pe.wait_ge(q_copied, a + 1)
                    if c is not None:
                        pe.wait_ge(pT_copied, c * 2 + 2)
                    for tt in range(TILES):
                        bank, off = (ps_s[0], SO[tt]) if tt < 2 else (ps_s[1], 0)
                        last = mm(bank[:, off:off + SW[tt]], qT[:, tt * P:(tt + 1) * P], xnT[:, 0:SW[tt]],
                                  start=True, stop=True)
                        if tt > 0:
                            last.then_inc(s_done, 1)
                if f is not None:
                    ffn2(1)
                if a is not None:
                    if c is not None:
                        pe.wait_ge(attn_added, c + 1)
                    for tt in range(TILES):
                        tile = ps_v[:, tt * P:(tt + 1) * P]
                        bias(tile, slice(D, 2 * D), True)
                        last = mm(tile, xnT[:, tt * P:(tt + 1) * P], w_vT[:, :], start=False, stop=True)
                    last.then_inc(v_done, 1)
                if t is not None:
                    pe.wait_ge(aff_ready, G * (t + 1))
                    if a is not None:
                        pe.wait_ge(max_ready, a + 1)
                    for tt in range(TILES):
                        n = P if tt < TILES - 1 else LAST
                        last = tr(ps_s[1][:, tt * P:tt * P + n], aff[0:n, tt, :, :].rearrange("p e g -> p (e g)"),
                                  ident[0:n, 0:n])
                    last.then_inc(aff_transposed, 1)

            steps(pe, step)

        @block.scalar
        def _(act):
            A = nc.scalar.activation
            act.wait_ge(weights_transposed, 1)
            A(w_tokT[:, :], ps[5][:, 0:CTX * D], ACT.Copy)
            A(w_vT[:, :], ps[6][:, 0:P], ACT.Copy)
            A(b1T[:, :], ps[6][:, P:P + E], ACT.Copy).then_inc(weights_ready, 1)

            def step(at):
                x, a, c, r, f = at.x, at.a, at.c, at.r, at.f

                def copy_gathered(half):
                    act.wait_ge(xg_transposed, f * 2 + half + 1)
                    A(xgT[half][:, :], ps_f[half][:, 0:SLOTS], ACT.Copy, scale=0.5).then_inc(xgT_copied, 1)

                def bias(half):
                    act.wait_ge(ffn1_done, f * 2 + half + 1)
                    act.wait_ge(pair_ready, f + 1)
                    if not first(f):
                        act.wait_ge(hid_ready, f * 2 + half - 1)
                    A(u[half][:, :], ps_f[half][:, 0:SLOTS], ACT.Identity, bias=half_b1[:, half:half + 1]) \
                        .then_inc(u_copied, 1)

                def square(half):
                    act.wait_ge(u_copied, f * 2 + half + 1)
                    A(u_sq[half][:, :], u[half][:, :], ACT.Square, scale=2.0 * GELU_C ** 0.5).then_inc(u_squared, 1)

                def tanh(half):
                    act.wait_ge(gelu_in_ready, f * 2 + half + 1)
                    A(tanh_out[half][:, :], gelu_in[half][:, :], ACT.Tanh, scale=2.0 * GELU_S).then_inc(tanh_done, 1)

                def weigh(half):
                    act.wait_ge(ffn2_done, f * 2 + half + 1)
                    act.wait_ge(table_ready, f + 1)
                    if not first(f):
                        act.wait_ge(scattered[half], f * 48)
                    for tt in range(TILES):
                        n = ROWS[tt]
                        last = A(y[half][0:n, tt, :], ps_y[0:n, tt * P:(tt + 1) * P], ACT.Copy,
                                 scale=gate[0:n, tt, half:half + 1])
                    last.then_inc(y_ready, 1)

                if x is not None:
                    act.wait_ge(x_transposed, x + 1)
                    A(xT[:, 0:NTOK], ps_x[:, 0:NTOK], ACT.Copy).then_inc(xT_copied, 1)
                if f is not None:
                    copy_gathered(0)
                if f is not None:
                    copy_gathered(1)
                if c is not None:
                    act.wait_ge(max_ready, c + 1)
                    for tt in range(TILES):
                        tile = probs[:, SO[tt]:SO[tt] + SW[tt]]
                        A(tile, tile, ACT.Exp, bias=neg_max[:, tt:tt + 1],
                          accum_out=row_sum[:, tt:tt + 1]).then_inc(exp_done, 1)
                if x is not None:
                    act.wait_ge(conv_done, x + 1)
                    if a is not None:
                        act.wait_ge(h_kept, a + 1)
                        act.wait_ge(xn_ready, a + 1)
                    A(h[:, :, :].rearrange("p a b -> p (a b)"), ps_x[:, 0:SP], ACT.Relu).then_inc(relu_done, 1)
                if a is not None:
                    act.wait_ge(xn_transposed, a + 1)
                    A(xnT[:, :], ps_q[:, 0:SP], ACT.Copy).then_inc(xnT_copied, 1)
                if c is not None:
                    for i in range(2):
                        act.wait_ge(pT_done, c * 2 + i + 1)
                        A(probsT[:, 3 * i:3 * i + 3, :].rearrange("p a b -> p (a b)"), ps_s[i][:, 0:SP],
                          ACT.Copy).then_inc(pT_copied, 1)
                if r is not None:
                    act.wait_ge(xn2_transposed, r + 1)
                    A(xn2T[:, :], ps_v[:, 0:SP], ACT.Copy).then_inc(xn2T_copied, 1)
                if f is not None:
                    bias(0)
                if f is not None:
                    square(0)
                if f is not None:
                    bias(1)
                if f is not None:
                    square(1)
                if a is not None:
                    act.wait_ge(q_done, a + 1)
                    A(qT[:, :], ps_q[:, 0:SP], ACT.Copy, scale=SCALE).then_inc(q_copied, 1)
                if r is not None:
                    act.wait_ge(logits_read, r + 1)
                    A(r_exp[:, :, :], r_exp[:, :, :], ACT.Exp).then_inc(r_exp_done, 1)
                if f is not None:
                    tanh(0)
                if f is not None:
                    tanh(1)
                if f is not None:
                    weigh(0)
                if a is not None:
                    act.wait_ge(v_done, a + 1)
                    A(v[:, :, :].rearrange("p a b -> p (a b)"), ps_v[:, 0:SP], ACT.Copy).then_inc(v_copied, 1)
                if f is not None:
                    weigh(1)

            steps(act, step)

        @block.vector
        def _(dve):
            V = nc.vector
            V.memset(bias_raw[:, :], 0.0).then_inc(vec_setup, 1)
            V.memset(bias_rows[:, :].bitcast(F32), 0.0).then_inc(vec_setup, 1)
            V.memset(xT[:, NTOK:XCOLS], 0.0).then_inc(vec_setup, 1)
            V.memset(ones_bf[:, :], 1.0).then_inc(vec_setup, 1)
            V.memset(ps_y[:, :], 0.0).then_inc(vec_setup, 1)
            V.memset(mv[:, :, :], 1.0).then_inc(vec_setup, 1)
            dve.wait_ge(pool_setup, 6)
            V.tensor_scalar(slot_base_i[:, :], slot_base_i[:, :], G - 1, None, ALU.bitwise_and).then_inc(vec_setup, 1)
            dve.wait_ge(vec_setup, 7)
            V.tensor_scalar(slot_base[:, :], slot_base_i[:, :], float(S), None, ALU.mult).then_inc(vec_setup, 1)
            dve.wait_ge(vec_setup, 8)
            dve.wait_ge(bias_loaded, 16 * 9)
            split_bias(V, slice(0, 2 * D), vec_split, bias_ready)
            dve.wait_ge(weights_ready, 1)

            def row_stats(src, side, done, count):
                for tt in range(TILES):
                    last = V.bn_stats(stats[:, side, tt, :], src[:, tt, :])
                last.then_inc(done, 1)
                dve.wait_ge(done, count)
                alone(dve)
                for tt in range(TILES):
                    last = V.bn_aggr(mv[:, side * TILES + tt, :], stats[:, side, tt, :])
                return last

            def step(at):
                x, a, c, r, t, f = at.x, at.a, at.c, at.r, at.t, at.f

                def next_indices(half):
                    if f is not None:
                        dve.wait_ge(gathered[half], f * 48 + 48)
                        alone(dve)
                    V.tensor_copy(gather_idx[:, half, :], tab_idx[:, :, bass.ds(at.next_expert + half, 1)]
                                  .rearrange("p a e -> p (a e)")).then_inc(gather_idx_ready[half], 1)

                def make_tables(g):
                    if f is not None:
                        dve.wait_ge(table_ready, f + 1)
                    dve.wait_ge(tab_transposed, g + 1)
                    tab = ps_y[:, 0:TILES * 2 * E].rearrange("p (a w e) -> p a w e", a=TILES, w=2)
                    V.tensor_copy(tab_idx[:, :, :], tab[:, :, 0, :])
                    V.tensor_copy(tab_gate[:, :, :], tab[:, :, 1, :]).then_inc(tab_ready, 1)
                    dve.wait_ge(tab_ready, g + 1)

                def scatter_table():
                    if not first(f):
                        dve.wait_ge(scattered[1], f * 48)
                        dve.wait_ge(y_ready, f * 2)
                        alone(dve)
                    V.tensor_copy(gate[:, :, :], tab_gate[:, :, bass.ds(at.expert, 2)])
                    V.tensor_scalar(scatter_idx[:, :, :], tab_idx[:, :, bass.ds(at.expert, 2)],
                                    float(at.f_group * G * S), None, ALU.add).then_inc(table_ready, 1)

                def gelu_argument(half):
                    dve.wait_ge(u_squared, f * 2 + half + 1)
                    V.scalar_tensor_tensor(gelu_in[half][:, :], u_sq[half][:, :], 1.0, u[half][:, :], ALU.add, ALU.mult) \
                        .then_inc(gelu_in_ready, 1)

                def hidden(half):
                    dve.wait_ge(tanh_done, f * 2 + half + 1)
                    if not first(f):
                        dve.wait_ge(ffn2_done, f * 2 + half - 1)
                    V.scalar_tensor_tensor(hidT[half][:, :], tanh_out[half][:, :], 1.0, u[half][:, :], ALU.add, ALU.mult) \
                        .then_inc(hid_ready, 1)

                def rsqrt(i):
                    if i:
                        dve.wait_ge(rsqrt_vec, at.j * 9 + i)
                    if i == 0:
                        ins = V.tensor_scalar(nv[:, :], mv[:, :, 1], EPS, -0.5, ALU.add, ALU.mult)
                    elif i == 1:
                        ins = V.tensor_scalar(rstd[:, :].bitcast(U32), nv[:, :].bitcast(U32), -0.5, RSQRT_MAGIC,
                                              ALU.mult, ALU.add)
                    elif i in (2, 6):
                        ins = V.tensor_tensor(sq[:, :], rstd[:, :], rstd[:, :], ALU.mult)
                    elif i in (3, 7):
                        ins = V.scalar_tensor_tensor(sq[:, :], sq[:, :], 1.0 if i == 3 else 3.375, nv[:, :],
                                                     ALU.mult, ALU.mult)
                    elif i == 4:
                        ins = V.scalar_tensor_tensor(sq[:, :], sq[:, :], 5.0 / 3.0, sq[:, :], ALU.add, ALU.mult)
                    else:
                        ins = V.scalar_tensor_tensor(rstd[:, :], sq[:, :], 1.25 if i == 5 else 2.25, rstd[:, :],
                                                     ALU.add, ALU.mult)
                    ins.then_inc(rsqrt_vec, 1)

                def normalise(src, dst, side):
                    for tt in range(TILES):
                        k = side * TILES + tt
                        last = V.tensor_scalar(dst[:, tt, :], src[:, tt, :], mv[:, k, 0:1], rstd[:, k:k + 1],
                                               ALU.subtract, ALU.mult)
                    return last

                norms = True if x is not None or c is not None else None
                logits = ps_v[:, SP:SP + TILES * E].rearrange("p (a e) -> p a e", a=TILES)

                def add_bias(tt):
                    bank, off = (ps_s[0], SO[tt]) if tt < 2 else (ps_s[1], 0)
                    dve.wait_ge(s_done, a * 2 + 1 + (tt == 2))
                    alone(dve)
                    return V.tensor_tensor_reduce(
                        out=probs[:, SO[tt]:SO[tt] + SW[tt]], in0=bank[:, off:off + SW[tt]],
                        in1=dist_bias[:, tt, 0:SW[tt]], scale=1.0, scalar=NEG, op0=ALU.add, op1=ALU.max,
                        accum_out=row_max[:, tt:tt + 1])

                if f is not None:
                    V.tensor_scalar(half_b1[:, :], b1T[:, bass.ds(at.expert, 2)], 0.5, None, ALU.mult) \
                        .then_inc(pair_ready, 1)
                if at.prepares and at.tables is None:
                    next_indices(0)
                    next_indices(1)
                if c is not None:
                    dve.wait_ge(h_kept, c + 1)
                    if not first(c):
                        dve.wait_ge(attn_added, c)
                    V.tensor_copy(hres[:, :, :], hnext[:, :, :]).then_inc(res_kept, 1)
                if a is not None:
                    if c is not None:
                        dve.wait_ge(res_kept, c + 1)
                    V.tensor_copy(hnext[:, :, :], h[:, :, :]).then_inc(h_kept, 1)
                if x is not None:
                    dve.wait_ge(relu_done, x + 1)
                    alone(dve)
                    row_stats(h, 0, x_vec, x + 1).then_inc(x_stats, 1)
                if c is not None:
                    dve.wait_ge(exp_done, c * 3 + 3)
                    V.reciprocal(row_inv[:, :], row_sum[:, :]).then_inc(c_vec, 1)
                if f is not None:
                    gelu_argument(0)
                if r is not None:
                    dve.wait_ge(logits_done, r + 1)
                    V.tensor_reduce(r_max[:, :, 0], logits, AX_X, ALU.max).then_inc(r_vec, 1)
                if r is not None:
                    dve.wait_ge(r_vec, r * 3 + 1)
                    V.tensor_tensor(r_exp[:, :, :], logits, r_max[:, :, :].to_broadcast([P, TILES, E]),
                                    ALU.subtract).then_inc(logits_read, 1)
                if f is not None:
                    gelu_argument(1)
                if c is not None:
                    dve.wait_ge(pv_done, c + 1)
                    dve.wait_ge(res_kept, c + 1)
                    dve.wait_ge(c_vec, c * 3 + 1)
                    if not first(c):
                        dve.wait_ge(rows_stored, c * 64)
                    for tt in range(TILES):
                        last = V.scalar_tensor_tensor(h2[:, tt, :], ps_v[:, tt * P:(tt + 1) * P],
                                                      row_inv[:, tt:tt + 1], hres[:, tt, :], ALU.mult, ALU.add)
                    last.then_inc(attn_added, 1)
                if f is not None:
                    scatter_table()
                if f is not None:
                    hidden(0)
                if r is not None:
                    dve.wait_ge(r_exp_done, r + 1)
                    V.tensor_reduce(r_sum[:, :, 0], r_exp[:, :, :], AX_X, ALU.add).then_inc(r_vec, 1)
                if at.tables is not None:
                    make_tables(at.tables)
                    next_indices(0)
                    next_indices(1)
                if f is not None:
                    hidden(1)
                if r is not None:
                    dve.wait_ge(r_vec, r * 3 + 2)
                    V.reciprocal(r_sum[:, :, :], r_sum[:, :, :]).then_inc(r_vec, 1)
                if c is not None:
                    dve.wait_ge(attn_added, c + 1)
                    alone(dve)
                    row_stats(h2, 1, c_vec, c * 3 + 2).then_inc(c_vec, 1)
                if norms is not None:
                    if x is not None:
                        dve.wait_ge(x_stats, x + 1)
                    if c is not None:
                        dve.wait_ge(c_vec, c * 3 + 3)
                    rsqrt(0)
                if r is not None:
                    dve.wait_ge(r_vec, r * 3 + 3)
                    V.tensor_tensor(aff[:, :, :, bass.ds(at.r_in_group, 1)].rearrange("p a e g -> p a (e g)"),
                                    r_exp[:, :, :], r_sum[:, :, :].to_broadcast([P, TILES, E]), ALU.mult) \
                        .then_inc(aff_ready, 1)
                if norms is not None:
                    rsqrt(1)
                if a is not None:
                    add_bias(0)
                if norms is not None:
                    rsqrt(2)
                if a is not None:
                    add_bias(1)
                if norms is not None:
                    rsqrt(3)
                if a is not None:
                    add_bias(2).then_inc(a_vec, 1)
                if norms is not None:
                    rsqrt(4)
                if a is not None:
                    dve.wait_ge(a_vec, a + 1)
                    V.tensor_scalar(neg_max[:, :], row_max[:, :], -1.0, None, ALU.mult).then_inc(max_ready, 1)
                if norms is not None:
                    rsqrt(5)
                if norms is not None:
                    rsqrt(6)
                if norms is not None:
                    rsqrt(7)
                if norms is not None:
                    rsqrt(8)
                if x is not None:
                    dve.wait_ge(rsqrt_vec, at.j * 9 + 9)
                    if not first(x):
                        dve.wait_ge(xn_transposed, x)
                    normalise(h, xn, 0).then_inc(xn_ready, 1)
                if c is not None:
                    dve.wait_ge(rsqrt_vec, at.j * 9 + 9)
                    if not first(c):
                        dve.wait_ge(xn2_transposed, c)
                    normalise(h2, xn2, 1).then_inc(xn2_ready, 1)
                if t is not None:
                    dve.wait_ge(aff_transposed, t + 1)
                    V.tensor_copy(affT[:, :], ps_s[1][:, 0:S]).then_inc(t_vec, 1)
                if t is not None:
                    seen = [t * 18 + 1]

                    def link(ins):
                        ins.then_inc(t_vec, 1)
                        seen[0] += 1
                    dve.wait_ge(t_vec, seen[0])
                    for k in range(ROUNDS):
                        top = top_val[:, 8 * k:8 * k + 8]
                        link(V.max(top, affT[:, :]))
                        dve.wait_ge(t_vec, seen[0])
                        link(V.max_index(top_idx[:, 8 * k:8 * k + 8], top, affT[:, :]))
                        if k < ROUNDS - 1:
                            dve.wait_ge(t_vec, seen[0])
                            link(V.match_replace(affT[:, :], top, affT[:, :], -1.0))
                        dve.wait_ge(t_vec, seen[0])
                    if t > 0:
                        dve.wait_ge(slots_stored, 16 * t)
                    V.tensor_scalar(slots[:, 0, :], top_idx[:, 0:CAP], slot_base[:, 0:1], None, ALU.add)
                    V.tensor_copy(slots[:, 1, :], top_val[:, 0:CAP]).then_inc(slots_ready, 1)

            steps(dve, step)


_INS = ["x", "L0_tok_weight", "L0_tok_bias", "L0_attn_W_qk", "L0_attn_W_v", "L0_attn_b_v", "L0_ffn_gate_weight",
        "L0_ffn_w1", "L0_ffn_b1", "L0_ffn_w2", "L0_ffn_b2"]


def kernel(**inputs):
    import numpy as _np
    import concourse.bacc as _bacc
    from concourse import mybir as _mybir
    from concourse.bass_utils import run_bass_kernel_spmd as _run

    nc = _bacc.Bacc("TRN2", target_bir_lowering=False, num_devices=1)
    arrays, args = {}, []
    for name in _INS:
        a = _np.ascontiguousarray(inputs[name])
        arrays[f"in_{name}"] = a
        args.append(nc.dram_tensor(f"in_{name}", a.shape, _mybir.dt.from_np(a.dtype), kind="ExternalInput").ap())
    batch, tokens, d = inputs["x"].shape
    rows = tokens - inputs["L0_tok_weight"].shape[1] // d + 1
    experts = inputs["L0_ffn_gate_weight"].shape[1]
    f32 = _mybir.dt.float32
    out = nc.dram_tensor("out_0", (batch, rows, d), f32, kind="ExternalOutput").ap()
    group = 128 // experts
    xn2_rows = [nc.dram_tensor(f"xn2_rows_{i}", (group * rows, d), f32).ap() for i in range(batch // group)]
    slots_dram = nc.dram_tensor("slots_scratch", (2, 128, rows // experts * 2), f32).ap()
    audio_tower_block(nc, *args, out, xn2_rows, slots_dram)
    r = _run(nc, [arrays], core_ids=[0])
    return r.results[0]["out_0"]
```

```python
from contextlib import ExitStack

import concourse.bass as bass
from concourse import mybir

F32 = mybir.dt.float32
BF16 = mybir.dt.bfloat16
I32 = mybir.dt.int32
U32 = mybir.dt.uint32
ALU = mybir.AluOpType
ACT = mybir.ActivationFunctionType
AX_X = mybir.AxisListType.X

P = 128
NEG = -3.0e38


class Step:

    def __init__(self, j, next_x, x, a, c, r, r_in_group, r_group, t, top_first, top_last, tables,
                 f, f_group, expert, next_expert, next_group, prepares, loads):
        self.j, self.next_x, self.x, self.a, self.c, self.r, self.f = j, next_x, x, a, c, r, f
        self.t, self.top_first, self.top_last, self.tables = t, top_first, top_last, tables
        self.r_in_group, self.r_group, self.f_group = r_in_group, r_group, f_group
        self.expert, self.next_expert, self.next_group = expert, next_expert, next_group
        self.prepares, self.loads = prepares, loads


def first(i):
    return isinstance(i, int) and i == 0


def audio_tower_block(nc, x, w_tok, b_tok, w_qk, w_v, b_v, w_gate, w1, b1, w2, b2, out, xn2_rows, slots_dram):
    B, NTOK, D = x.shape
    CTX = w_tok.shape[1] // D
    S = NTOK - CTX + 1
    E = w_gate.shape[1]
    CAP = S // E * 2
    TILES = -(-S // P)
    SP = TILES * P
    LAST = S - (TILES - 1) * P
    LASTX = NTOK - (TILES - 1) * P
    G = P // E
    GROUPS = B // G
    SLOTS = G * CAP
    ROUNDS = -(-CAP // 8)
    LAST_SLOTS = SLOTS - 2 * P
    PAIRS = E // 2
    NF = GROUPS * PAIRS
    SCALE = float(D) ** -0.5
    EPS = 1e-5
    SLOPE = 0.5
    GELU_C = 0.044715
    GELU_S = 0.7978845608028654
    RSQRT_MAGIC = 1597463007.0 + 0.5 * (2.0 ** 31 - 2.0 ** 23) - 2.0 ** 31
    assert ROUNDS == 6 and TILES == 3 and D == P and G * E == P and SLOTS <= 3 * P and G == PAIRS
    XCOLS = (TILES - 1) * P + P + CTX - 1
    ROWS = [P, P, LAST_SLOTS]
    SW = [P * (t + 1) for t in range(TILES)]
    SO = [0, P, 3 * P]

    out_rows = out.rearrange("b s d -> (b s) d")
    x_rows = x.rearrange("b s d -> (b s) d")

    with ExitStack() as ctx:
        def sb(name, shape, dt=F32):
            return ctx.enter_context(nc.sbuf_tensor(name, shape, dt))

        def sem(name):
            return ctx.enter_context(nc.semaphore(name))

        ident = sb("ident", [P, P])
        dist_bias = sb("dist_bias", [P, TILES, SP])
        w_tok_raw = sb("w_tok_raw", [P, CTX * D])
        w_v_raw = sb("w_v_raw", [P, D])
        b1_raw = sb("b1_raw", [E, D])
        w_tokT = sb("w_tokT", [P, CTX * D])
        w_vT = sb("w_vT", [P, D])
        b1T = sb("b1T", [P, E])
        w_qk_sb = sb("w_qk_sb", [P, D])
        w_gate_sb = sb("w_gate_sb", [P, E])
        bias_raw = sb("bias_raw", [96, (2 + E) * D])
        bias_parts = sb("bias_parts", [96, 2, (2 + E) * D], BF16)
        bias_rows = sb("bias_rows", [96, (2 + E) * D], BF16)
        ones_bf = sb("ones_bf", [96, P], BF16)
        slot_base = sb("slot_base", [P, 1])
        slot_base_i = sb("slot_base_i", [P, 1], I32)
        xs = sb("xs", [P, TILES, D])
        xT = sb("xT", [P, XCOLS])
        h = sb("h", [P, TILES, D])
        xn = sb("xn", [P, TILES, D])
        hres = sb("hres", [P, TILES, D])
        hnext = sb("hnext", [P, TILES, D])
        xnT = sb("xnT", [P, SP])
        qT = sb("qT", [P, SP])
        v = sb("v", [P, TILES, D])
        probs = sb("probs", [P, 6 * P])
        row_max = sb("row_max", [P, TILES])
        neg_max = sb("neg_max", [P, TILES])
        row_sum = sb("row_sum", [P, TILES])
        row_inv = sb("row_inv", [P, TILES])
        probsT = sb("probsT", [P, 6, P])
        h2 = sb("h2", [P, TILES, D])
        xn2 = sb("xn2", [P, TILES, D])
        stats = sb("stats", [P, 2, TILES, 6])
        mv = sb("mv", [P, 2 * TILES, 2])
        nv = sb("nv", [P, 2 * TILES])
        rstd = sb("rstd", [P, 2 * TILES])
        sq = sb("sq", [P, 2 * TILES])
        xn2T = sb("xn2T", [P, SP])
        r_max = sb("r_max", [P, TILES, 1])
        r_exp = sb("r_exp", [P, TILES, E])
        r_sum = sb("r_sum", [P, TILES, 1])
        aff = sb("aff", [P, TILES, E, G])
        affT = sb("affT", [P, S])
        top_val = sb("top_val", [P, 8 * ROUNDS])
        top_idx = sb("top_idx", [P, 8 * ROUNDS], U32)
        slots = sb("slots", [P, 2, CAP])
        slot_rows = sb("slot_rows", [2 * E, SLOTS])
        tab_idx = [sb(f"tab_idx_{i}", [P, TILES, E], I32) for i in range(2)]
        tab_gate = [sb(f"tab_gate_{i}", [P, TILES, E]) for i in range(2)]
        gather_idx = sb("gather_idx", [P, 2, TILES], I32)
        scatter_idx = sb("scatter_idx", [P, 2, TILES], I32)
        gate = sb("gate", [P, 2, TILES])
        half_b1 = sb("half_b1", [P, 2])
        w1_sb = [sb(f"w1_{i}", [P, D]) for i in "ab"]
        w2_sb = [sb(f"w2_{i}", [P, D]) for i in "ab"]
        xg = [sb(f"xg_{i}", [P, TILES, D]) for i in "ab"]
        y = [sb(f"y_{i}", [P, TILES, D]) for i in "ab"]
        xgT = [sb(f"xgT_{i}", [P, SLOTS]) for i in "ab"]
        u = [sb(f"u_{i}", [P, SLOTS]) for i in "ab"]
        u_sq = [sb(f"u_sq_{i}", [P, SLOTS]) for i in "ab"]
        gelu_in = [sb(f"gelu_in_{i}", [P, SLOTS]) for i in "ab"]
        tanh_out = [sb(f"tanh_out_{i}", [P, SLOTS]) for i in "ab"]
        hidT = [sb(f"hidT_{i}", [P, SLOTS]) for i in "ab"]

        ps = [ctx.enter_context(nc.psum_tensor(f"bank{i}", [P, 512], F32)) for i in range(8)]
        ps_x = ps[1]
        ps_q = ps[0]
        ps_v = ps[2]
        ps_s = [ps[3], ps[4]]
        ps_f = [ps[5], ps[6]]
        ps_y = ps[7]

        w_tok_loaded = sem("w_tok_loaded")
        consts_loaded = sem("consts_loaded")
        pool_setup = sem("pool_setup")
        vec_setup = sem("vec_setup")
        weights_transposed = sem("weights_transposed")
        weights_ready = sem("weights_ready")
        x_loaded = sem("x_loaded")
        x_transposed = sem("x_transposed")
        xT_copied = sem("xT_copied")
        conv_done = sem("conv_done")
        relu_done = sem("relu_done")
        x_vec = sem("x_vec")
        x_stats = sem("x_stats")
        h_kept = sem("h_kept")
        res_kept = sem("res_kept")
        v_copied = sem("v_copied")
        a_vec = sem("a_vec")
        c_vec = sem("c_vec")
        rsqrt_vec = sem("rsqrt_vec")
        bias_loaded = sem("bias_loaded")
        bias_ready = sem("bias_ready")
        b2_loaded = sem("b2_loaded")
        late_consts_loaded = sem("late_consts_loaded")
        b2_ready = sem("b2_ready")
        vec_split = sem("vec_split")
        pool_split = sem("pool_split")
        xn_ready = sem("xn_ready")
        xn_transposed = sem("xn_transposed")
        xnT_copied = sem("xnT_copied")
        q_done = sem("q_done")
        q_copied = sem("q_copied")
        v_done = sem("v_done")
        s_done = sem("s_done")
        max_ready = sem("max_ready")
        exp_done = sem("exp_done")
        pT_done = sem("pT_done")
        pT_copied = sem("pT_copied")
        pv_done = sem("pv_done")
        attn_added = sem("attn_added")
        xn2_ready = sem("xn2_ready")
        rows_stored = sem("rows_stored")
        xn2_transposed = sem("xn2_transposed")
        xn2T_copied = sem("xn2T_copied")
        logits_done = sem("logits_done")
        logits_read = sem("logits_read")
        r_exp_done = sem("r_exp_done")
        r_vec = sem("r_vec")
        aff_ready = sem("aff_ready")
        aff_transposed = sem("aff_transposed")
        t_vec = sem("t_vec")
        slots_ready = sem("slots_ready")
        slots_stored = sem("slots_stored")
        slots_loaded = sem("slots_loaded")
        tab_transposed = sem("tab_transposed")
        tab_ready = sem("tab_ready")
        gather_idx_ready = [sem(f"gather_idx_ready_{i}") for i in "ab"]
        pair_ready = sem("pair_ready")
        table_ready = [sem(f"table_ready_{i}") for i in "ab"]
        gathered = [sem(f"gathered_{i}") for i in "ab"]
        scattered = [sem(f"scattered_{i}") for i in "ab"]
        w1_loaded = [sem(f"w1_loaded_{i}") for i in "ab"]
        w2_loaded = [sem(f"w2_loaded_{i}") for i in "ab"]
        xg_transposed = sem("xg_transposed")
        xgT_copied = sem("xgT_copied")
        ffn1_done = sem("ffn1_done")
        u_copied = sem("u_copied")
        u_squared = sem("u_squared")
        gelu_in_ready = sem("gelu_in_ready")
        tanh_done = sem("tanh_done")
        hid_ready = sem("hid_ready")
        ffn2_done = sem("ffn2_done")
        y_ready = sem("y_ready")

        spacer = [sem("spacer_pool"), sem("spacer_vec")]

        block = ctx.enter_context(nc.Block())

        def steps(eng, step):
            last = B + 5 + PAIRS

            def one(j, lo):
                step(Step(
                    j=j,
                    next_x=j + 1 if lo + 1 < B else None,
                    x=j if lo < B else None,
                    a=j - 1 if 1 <= lo <= B else None,
                    c=j - 2 if 2 <= lo <= B + 1 else None,
                    r=j - 3 if 3 <= lo <= B + 2 else None,
                    r_in_group=(lo - 3) % G + (j - lo),
                    r_group=(lo - 3) // G,
                    t=(lo - 10) // G if 10 <= lo <= B + 2 and (lo - 10) % G == 0 else None,
                    top_first=(lo - 11) // G if 11 <= lo <= B + 3 and (lo - 11) % G == 0 else None,
                    top_last=(lo - 12) // G if 12 <= lo <= B + 4 and (lo - 12) % G == 0 else None,
                    tables=(lo - 13) // G if 13 <= lo <= B + 5 and (lo - 13) % G == 0 else None,
                    f=j - 14 if lo >= 14 else None,
                    f_group=(lo - 14) // PAIRS,
                    expert=2 * ((lo - 14) % PAIRS + (j - lo)),
                    next_expert=2 * ((lo - 13) % PAIRS + (j - lo)),
                    next_group=(lo - 13) // PAIRS,
                    prepares=13 <= lo < last,
                    loads=lo + 2 < B))

            starts = (0, 1, 2, 3, 10, 11, 12, 13, 14, 15, 16, 18, 19, 20, 21, 22, 26, 27, 28, 29, 30, 31, 32, 33, 34,
                      35, 36, 37, 38, last, last + 1)
            for lo, hi in zip(starts, starts[1:]):
                if hi - lo == 1:
                    one(lo, lo)
                else:
                    with eng.Fori(lo, hi) as j:
                        one(j, lo)

        def split_bias(eng, cols, done, ready):
            raw, rows = bias_raw[:, cols], bias_rows[:, cols]
            p1, p2 = (bias_parts[:, k, cols] for k in range(2))
            eng.tensor_copy(p1, raw).then_inc(done, 1)
            eng.wait_ge(done, 1)
            eng.tensor_copy(rows[0:1, :], p1[0:1, :]).then_inc(done, 1)
            eng.wait_ge(done, 2)
            eng.tensor_tensor(raw, raw, p1, ALU.subtract).then_inc(done, 1)
            eng.wait_ge(done, 3)
            eng.tensor_copy(p2, raw).then_inc(done, 1)
            eng.wait_ge(done, 4)
            eng.tensor_copy(rows[32:33, :], p2[32:33, :]).then_inc(done, 1)
            eng.wait_ge(done, 5)
            eng.tensor_tensor(raw, raw, p2, ALU.subtract).then_inc(done, 1)
            eng.wait_ge(done, 6)
            eng.tensor_copy(rows[64:65, :], raw[64:65, :]).then_inc(ready, 1)

        def alone(eng):
            eng.sem_inc(spacer[0 if eng is nc.gpsimd else 1], 1)

        @block.sync
        def _(sp):
            def load_x(b):
                r = b * NTOK
                sp.dma_start(xs[:, 0:2, :], x_rows[bass.ds(r, 2 * P), :].rearrange("(t p) d -> p t d", p=P)) \
                    .then_inc(x_loaded, 16)
                sp.dma_start(xs[0:LASTX, 2, :], x_rows[bass.ds(r + 2 * P, LASTX), :]).then_inc(x_loaded, 16)

            def store_rows(b, in_group, g):
                for dst, r, src in ((out_rows, b * S, h2), (xn2_rows[g], in_group * S, xn2)):
                    sp.dma_start(dst[bass.ds(r, 2 * P), :].rearrange("(t p) d -> p t d", p=P), src[:, 0:2, :]) \
                        .then_inc(rows_stored, 16)
                    sp.dma_start(dst[bass.ds(r + 2 * P, LAST), :], src[0:LAST, 2, :]).then_inc(rows_stored, 16)

            def step(at):
                def load(weights, buf, loaded, half, used):
                    if at.f is not None:
                        sp.wait_ge(used, at.f * 2 + half + 1)
                    sp.dma_start(buf[half][:, :], weights[bass.ds(at.next_expert + half, 1)]
                                 .rearrange("a d n -> (a d) n")).then_inc(loaded[half], 16)

                if at.r is not None:
                    sp.wait_ge(xn2_ready, at.r + 1)
                    if not first(at.r):
                        sp.wait_ge(rows_stored, at.r * 64)
                    store_rows(at.r, at.r_in_group, at.r_group)
                if at.next_x is not None and at.loads:
                    sp.wait_ge(x_transposed, at.next_x + 1)
                    load_x(at.next_x + 1)
                if at.prepares:
                    load(w1, w1_sb, w1_loaded, 0, ffn1_done)
                    load(w1, w1_sb, w1_loaded, 1, ffn1_done)
                if at.top_last is not None:
                    sp.wait_ge(slots_ready, at.top_last + 1)
                    sp.dma_start(slots_dram.rearrange("w p s -> p w s"), slots[:, :, :]).then_inc(slots_stored, 16)
                    sp.wait_ge(slots_stored, 16 * (at.top_last + 1))
                    sp.dma_start(slot_rows[:, :], slots_dram.rearrange("w (e g) s -> (w e) (g s)", g=G)) \
                        .then_inc(slots_loaded, 16)
                if at.prepares:
                    load(w2, w2_sb, w2_loaded, 0, ffn2_done)
                    load(w2, w2_sb, w2_loaded, 1, ffn2_done)

            sp.dma_start(w_tok_raw[:, :], w_tok).then_inc(w_tok_loaded, 16)
            load_x(0)
            sp.wait_ge(vec_setup, 1)
            for part in range(3):
                for col, src in ((0, b_tok.rearrange("(a d) -> a d", a=1)), (D, b_v.rearrange("(a d) -> a d", a=1))):
                    sp.dma_start(bias_raw[32 * part:32 * part + 1, col:col + D], src).then_inc(bias_loaded, 16)
            for dst, src in ((w_v_raw[:, :], w_v), (b1_raw[:, :], b1)):
                sp.dma_start(dst, src).then_inc(consts_loaded, 16)
            for dst, src in ((w_qk_sb[:, :], w_qk), (w_gate_sb[:, :], w_gate)):
                sp.dma_start(dst, src).then_inc(late_consts_loaded, 16)
            sp.wait_ge(x_transposed, 1)
            load_x(1)
            sp.wait_ge(pool_setup, 7)
            for part in range(3):
                sp.dma_start(bias_raw[32 * part:32 * part + 1, 2 * D:], b2.rearrange("(a e) d -> a (e d)", a=1)) \
                    .then_inc(b2_loaded, 16)
            steps(sp, step)
            sp.wait_ge(scattered[1], NF * 48)

        @block.gpsimd
        def _(pool):
            pool.memset(ident[:, :], 0.0).then_inc(pool_setup, 1)
            pool.iota(slot_base_i[:, :], pattern=[[0, 1]], base=0, channel_multiplier=1).then_inc(pool_setup, 1)
            pool.wait_ge(pool_setup, 2)
            pool.affine_select(out=ident[:, :], in_=ident[:, :], compare_op=ALU.not_equal, fill=1.0, base=0,
                               pattern=[[-1, P]], channel_multiplier=1).then_inc(pool_setup, 1)
            pool.iota(dist_bias[:, :, :], pattern=[[-P, TILES], [1, SP]], base=0, channel_multiplier=-1,
                      allow_small_or_imprecise_dtypes=True).then_inc(pool_setup, 1)
            pool.wait_ge(pool_setup, 4)
            pool.tensor_scalar(dist_bias[:, :, :], dist_bias[:, :, :], SLOPE, None, ALU.mult).then_inc(pool_setup, 1)
            pool.wait_ge(pool_setup, 5)
            pool.affine_select(out=dist_bias[:, :, :], in_=dist_bias[:, :, :], compare_op=ALU.is_ge, fill=NEG, base=0,
                               pattern=[[P, TILES], [-1, SP]], channel_multiplier=1).then_inc(pool_setup, 1)
            pool.wait_ge(pool_setup, 6)

            pool.memset(bias_raw[:, 2 * D:], 0.0).then_inc(pool_setup, 1)
            pool.wait_ge(pool_setup, 7)
            pool.memset(bias_rows[:, 2 * D:].bitcast(F32), 0.0).then_inc(pool_setup, 1)
            pool.wait_ge(pool_setup, 8)
            pool.wait_ge(b2_loaded, 16 * 3)
            split_bias(pool, slice(2 * D, (2 + E) * D), pool_split, b2_ready)
            pool.wait_ge(b2_ready, 1)

            def gather(f, half, g):
                pool.wait_ge(gather_idx_ready[half], f + 1)
                if not first(f):
                    pool.wait_ge(xg_transposed, f * 2 - 1 + half)
                alone(pool)
                for tt in range(TILES):
                    n = ROWS[tt]
                    pool.indirect_dma_start(
                        out=xg[half][0:n, tt, :], out_offset=None, in_=xn2_rows[g],
                        in_offset=bass.IndirectOffsetOnAxis(ap=gather_idx[0:n, half, tt:tt + 1], axis=0)) \
                        .then_inc(gathered[half], 16)

            def scatter(f, half):
                pool.wait_ge(y_ready, f * 2 + half + 1)
                pool.wait_ge(table_ready[half], f + 1)
                if half:
                    pool.wait_ge(scattered[0], f * 48 + 48)
                elif not first(f):
                    pool.wait_ge(scattered[1], f * 48)
                alone(pool)
                for tt in range(TILES):
                    n = ROWS[tt]
                    pool.indirect_dma_start(
                        out=out_rows,
                        out_offset=bass.IndirectOffsetOnAxis(ap=scatter_idx[0:n, half, tt:tt + 1], axis=0),
                        in_=y[half][0:n, tt, :], in_offset=None, compute_op=ALU.add) \
                        .then_inc(scattered[half], 16)

            def step(at):
                if at.tables is not None:
                    pool.wait_ge(rows_stored, 64 * G * (at.tables + 1))
                if at.prepares:
                    gather(0 if at.f is None else at.f + 1, 0, at.next_group)
                if at.f is not None and not first(at.f):
                    scatter(at.f - 1, 1)
                if at.prepares:
                    gather(0 if at.f is None else at.f + 1, 1, at.next_group)
                if at.f is not None:
                    scatter(at.f, 0)

            steps(pool, step)
            scatter(NF - 1, 1)
            pool.wait_ge(scattered[0], NF * 48)
            pool.wait_ge(scattered[1], NF * 48)

        @block.tensor
        def _(pe):
            mm, tr = nc.tensor.matmul, nc.tensor.transpose
            pe.wait_ge(pool_setup, 3)
            pe.wait_ge(w_tok_loaded, 16)
            pe.wait_ge(vec_setup, 5)
            for c in range(CTX):
                last = tr(ps[5][:, c * P:(c + 1) * P], w_tok_raw[:, c * P:(c + 1) * P], ident[:, :])
            last.then_inc(weights_transposed, 1)

            def bias(out_ap, col, start):
                return mm(out_ap, ones_bf[:, 0:out_ap.shape[0]], bias_rows[:, col], start=start, stop=False)

            def transpose_x(x):
                pe.wait_ge(x_loaded, x * 32 + 32)
                if not first(x):
                    pe.wait_ge(relu_done, x)
                for tt in range(TILES):
                    n = P if tt < TILES - 1 else LASTX
                    last = tr(ps_x[:, tt * P:tt * P + n], xs[0:n, tt, :], ident[0:n, 0:n])
                last.then_inc(x_transposed, 1)

            def project(x):
                pe.wait_ge(xT_copied, x + 1)
                if first(x):
                    pe.wait_ge(bias_ready, 1)
                for tt in range(TILES):
                    tile = ps_x[:, tt * P:(tt + 1) * P]
                    bias(tile, slice(0, D), True)
                    for k in range(CTX):
                        last = mm(tile, xT[:, tt * P + k:tt * P + k + P], w_tokT[:, k * D:(k + 1) * D],
                                  start=False, stop=(k == CTX - 1))
                last.then_inc(conv_done, 1)

            transpose_x(0)
            pe.wait_ge(consts_loaded, 16 * 2)
            tr(ps[6][:, 0:P], w_v_raw[:, :], ident[:, :])
            tr(ps[6][:, P:P + E], b1_raw[:, :], ident[0:E, 0:E]).then_inc(weights_transposed, 1)
            pe.wait_ge(weights_ready, 1)
            project(0)
            pe.wait_ge(weights_ready, 2)

            def step(at):
                x, a, c, r, t, f = at.x, at.a, at.c, at.r, at.t, at.f

                def transpose_probs(i):
                    pe.wait_ge(exp_done, c * 3 + 2 + i)
                    if i == 1 and at.top_first is not None:
                        pe.wait_ge(t_vec, 18 * at.top_first + 1)
                    for tt in ((0, 1), (2,))[i]:
                        off = SO[tt] if i == 0 else 0
                        for k in range(tt + 1):
                            last = tr(ps_s[i][:, off + k * P:off + (k + 1) * P],
                                      probs[:, SO[tt] + k * P:SO[tt] + (k + 1) * P], ident[:, :])
                    last.then_inc(pT_done, 1)

                def scores(i):
                    pe.wait_ge(q_copied, a + 1)
                    if c is not None:
                        pe.wait_ge(pT_copied, c * 2 + 1 + i)
                    for tt in ((0, 1), (2,))[i]:
                        off = SO[tt] if i == 0 else 0
                        last = mm(ps_s[i][:, off:off + SW[tt]], qT[:, tt * P:(tt + 1) * P], xnT[:, 0:SW[tt]],
                                  start=True, stop=True)
                    last.then_inc(s_done, 1)

                def gather_transpose(half):
                    pe.wait_ge(gathered[half], f * 48 + 48)
                    if not first(f):
                        pe.wait_ge(u_copied, f * 2 + half - 1)
                    for tt in range(TILES):
                        n = ROWS[tt]
                        last = tr(ps_f[half][:, tt * P:tt * P + n], xg[half][0:n, tt, :], ident[0:n, 0:n])
                    last.then_inc(xg_transposed, 1)

                def ffn1(half):
                    pe.wait_ge(xgT_copied, f * 2 + half + 1)
                    pe.wait_ge(w1_loaded[half], f * 16 + 16)
                    mm(ps_f[half][:, 0:SLOTS], w1_sb[half][:, :], xgT[half][:, :], start=True, stop=True) \
                        .then_inc(ffn1_done, 1)

                def ffn2(half):
                    pe.wait_ge(hid_ready, f * 2 + half + 1)
                    pe.wait_ge(w2_loaded[half], f * 16 + 16)
                    if not (first(f) and half == 0):
                        pe.wait_ge(y_ready, f * 2 + half)
                    for tt in range(TILES):
                        n = ROWS[tt]
                        tile = ps_y[0:n, tt * P:(tt + 1) * P]
                        bias(tile, bass.ds((at.expert + half + 2) * D, D), True)
                        last = mm(tile, hidT[half][:, tt * P:tt * P + n], w2_sb[half][:, :], start=False, stop=True)
                    last.then_inc(ffn2_done, 1)

                if r is not None:
                    pe.wait_ge(xn2_ready, r + 1)
                    pe.wait_ge(attn_added, r + 1)
                    if c is not None:
                        pe.wait_ge(v_copied, c + 1)
                    for tt in range(TILES):
                        last = tr(ps_v[:, tt * P:(tt + 1) * P], xn2[:, tt, :], ident[:, :])
                    last.then_inc(xn2_transposed, 1)
                if f is not None:
                    gather_transpose(0)
                if c is not None:
                    transpose_probs(0)
                    transpose_probs(1)
                if r is not None:
                    pe.wait_ge(xn2T_copied, r + 1)
                    if not first(r):
                        pe.wait_ge(logits_read, r)
                    for tt in range(TILES):
                        last = mm(ps_v[:, SP + tt * E:SP + (tt + 1) * E], xn2T[:, tt * P:(tt + 1) * P],
                                  w_gate_sb[:, :], start=True, stop=True)
                    last.then_inc(logits_done, 1)
                if at.tables is not None:
                    pe.wait_ge(slots_loaded, 16 * (at.tables + 1))
                    if c is not None:
                        pe.wait_ge(q_copied, c + 1)
                    for tt in range(TILES):
                        n = ROWS[tt]
                        last = tr(ps_q[0:n, tt * 2 * E:(tt + 1) * 2 * E], slot_rows[:, tt * P:tt * P + n],
                                  ident[0:2 * E, 0:2 * E])
                    last.then_inc(tab_transposed, 1)
                if a is not None:
                    pe.wait_ge(xn_ready, a + 1)
                    if at.tables is not None:
                        pe.wait_ge(tab_ready, at.tables + 1)
                    if not first(a):
                        pe.wait_ge(q_copied, a)
                    for tt in range(TILES):
                        last = tr(ps_q[:, tt * P:(tt + 1) * P], xn[:, tt, :], ident[:, :])
                    last.then_inc(xn_transposed, 1)
                if f is not None:
                    ffn1(0)
                    gather_transpose(1)
                if c is not None:
                    if r is not None:
                        pe.wait_ge(logits_read, r + 1)
                    pe.wait_ge(v_copied, c + 1)
                    pe.wait_ge(pT_copied, c * 2 + 2)
                    for tt in range(TILES):
                        for k in range(tt + 1):
                            last = mm(ps_v[:, tt * P:(tt + 1) * P], probsT[:, SO[tt] // P + k, :], v[:, k, :],
                                      start=(k == 0), stop=(k == tt))
                    last.then_inc(pv_done, 1)
                if a is not None:
                    pe.wait_ge(xnT_copied, a + 1)
                    if first(a):
                        pe.wait_ge(late_consts_loaded, 16 * 2)
                    mm(ps_q[:, 0:SP], w_qk_sb[:, :], xnT[:, :], start=True, stop=True).then_inc(q_done, 1)
                if f is not None:
                    ffn1(1)
                if at.next_x is not None:
                    transpose_x(at.next_x)
                if a is not None:
                    scores(0)
                    scores(1)
                    if c is not None:
                        pe.wait_ge(attn_added, c + 1)
                    for tt in range(TILES):
                        tile = ps_v[:, tt * P:(tt + 1) * P]
                        bias(tile, slice(D, 2 * D), True)
                        last = mm(tile, xnT[:, tt * P:(tt + 1) * P], w_vT[:, :], start=False, stop=True)
                    last.then_inc(v_done, 1)
                if f is not None:
                    if first(f):
                        pe.wait_ge(b2_ready, 1)
                    ffn2(0)
                if at.next_x is not None:
                    project(at.next_x)
                if f is not None:
                    ffn2(1)
                if t is not None:
                    pe.wait_ge(aff_ready, G * (t + 1))
                    if a is not None:
                        pe.wait_ge(max_ready, a + 1)
                    for tt in range(TILES):
                        n = P if tt < TILES - 1 else LAST
                        last = tr(ps_s[1][:, tt * P:tt * P + n], aff[0:n, tt, :, :].rearrange("p e g -> p (e g)"),
                                  ident[0:n, 0:n])
                    last.then_inc(aff_transposed, 1)

            steps(pe, step)

        @block.scalar
        def _(act):
            A = nc.scalar.activation
            act.wait_ge(weights_transposed, 1)
            A(w_tokT[:, :], ps[5][:, 0:CTX * D], ACT.Copy).then_inc(weights_ready, 1)

            def copy_x(x):
                act.wait_ge(x_transposed, x + 1)
                A(xT[:, 0:NTOK], ps_x[:, 0:NTOK], ACT.Copy).then_inc(xT_copied, 1)

            def weigh(f, half):
                act.wait_ge(ffn2_done, f * 2 + half + 1)
                act.wait_ge(table_ready[half], f + 1)
                if not first(f):
                    act.wait_ge(scattered[half], f * 48)
                for tt in range(TILES):
                    n = ROWS[tt]
                    last = A(y[half][0:n, tt, :], ps_y[0:n, tt * P:(tt + 1) * P], ACT.Copy,
                             scale=gate[0:n, half, tt:tt + 1])
                last.then_inc(y_ready, 1)

            copy_x(0)
            act.wait_ge(weights_transposed, 2)
            A(w_vT[:, :], ps[6][:, 0:P], ACT.Copy)
            A(b1T[:, :], ps[6][:, P:P + E], ACT.Copy).then_inc(weights_ready, 1)

            def step(at):
                x, a, c, r, f = at.x, at.a, at.c, at.r, at.f

                def copy_probs(i):
                    act.wait_ge(pT_done, c * 2 + i + 1)
                    A(probsT[:, 3 * i:3 * i + 3, :].rearrange("p a b -> p (a b)"), ps_s[i][:, 0:SP],
                      ACT.Copy).then_inc(pT_copied, 1)

                def copy_gathered(half):
                    act.wait_ge(xg_transposed, f * 2 + half + 1)
                    A(xgT[half][:, :], ps_f[half][:, 0:SLOTS], ACT.Copy, scale=0.5).then_inc(xgT_copied, 1)

                def bias(half):
                    act.wait_ge(ffn1_done, f * 2 + half + 1)
                    act.wait_ge(pair_ready, f + 1)
                    if not first(f):
                        act.wait_ge(hid_ready, f * 2 + half - 1)
                    A(u[half][:, :], ps_f[half][:, 0:SLOTS], ACT.Identity, bias=half_b1[:, half:half + 1]) \
                        .then_inc(u_copied, 1)

                def square(half):
                    act.wait_ge(u_copied, f * 2 + half + 1)
                    A(u_sq[half][:, :], u[half][:, :], ACT.Square, scale=2.0 * GELU_C ** 0.5).then_inc(u_squared, 1)

                def tanh(half):
                    act.wait_ge(gelu_in_ready, f * 2 + half + 1)
                    A(tanh_out[half][:, :], gelu_in[half][:, :], ACT.Tanh, scale=2.0 * GELU_S).then_inc(tanh_done, 1)

                if c is not None:
                    act.wait_ge(max_ready, c + 1)
                    for tt in range(TILES):
                        tile = probs[:, SO[tt]:SO[tt] + SW[tt]]
                        A(tile, tile, ACT.Exp, bias=neg_max[:, tt:tt + 1],
                          accum_out=row_sum[:, tt:tt + 1]).then_inc(exp_done, 1)
                if r is not None:
                    act.wait_ge(xn2_transposed, r + 1)
                    A(xn2T[:, :], ps_v[:, 0:SP], ACT.Copy).then_inc(xn2T_copied, 1)
                if f is not None:
                    copy_gathered(0)
                if c is not None:
                    copy_probs(0)
                    copy_probs(1)
                if x is not None:
                    act.wait_ge(conv_done, x + 1)
                    if a is not None:
                        act.wait_ge(h_kept, a + 1)
                        act.wait_ge(xn_ready, a + 1)
                    A(h[:, :, :].rearrange("p a b -> p (a b)"), ps_x[:, 0:SP], ACT.Relu).then_inc(relu_done, 1)
                if f is not None and not first(f):
                    weigh(f - 1, 1)
                if a is not None:
                    act.wait_ge(xn_transposed, a + 1)
                    A(xnT[:, :], ps_q[:, 0:SP], ACT.Copy).then_inc(xnT_copied, 1)
                if f is not None:
                    copy_gathered(1)
                    bias(0)
                    square(0)
                if a is not None:
                    act.wait_ge(q_done, a + 1)
                    A(qT[:, :], ps_q[:, 0:SP], ACT.Copy, scale=SCALE).then_inc(q_copied, 1)
                if f is not None:
                    tanh(0)
                    bias(1)
                if r is not None:
                    act.wait_ge(logits_read, r + 1)
                    A(r_exp[:, :, :], r_exp[:, :, :], ACT.Exp).then_inc(r_exp_done, 1)
                if f is not None:
                    square(1)
                if at.next_x is not None:
                    copy_x(at.next_x)
                if f is not None:
                    tanh(1)
                if a is not None:
                    act.wait_ge(v_done, a + 1)
                    A(v[:, :, :].rearrange("p a b -> p (a b)"), ps_v[:, 0:SP], ACT.Copy).then_inc(v_copied, 1)
                if f is not None:
                    weigh(f, 0)

            steps(act, step)
            weigh(NF - 1, 1)

        @block.vector
        def _(dve):
            V = nc.vector
            V.memset(bias_raw[:, 0:2 * D], 0.0).then_inc(vec_setup, 1)
            V.memset(bias_rows[:, 0:2 * D].bitcast(F32), 0.0).then_inc(vec_setup, 1)
            V.memset(xT[:, NTOK:XCOLS], 0.0).then_inc(vec_setup, 1)
            V.memset(ones_bf[:, :], 1.0).then_inc(vec_setup, 1)
            V.memset(ps_y[:, :], 0.0).then_inc(vec_setup, 1)
            V.memset(mv[:, :, :], 1.0).then_inc(vec_setup, 1)
            dve.wait_ge(pool_setup, 2)
            V.tensor_scalar(slot_base_i[:, :], slot_base_i[:, :], G - 1, None, ALU.bitwise_and).then_inc(vec_setup, 1)
            dve.wait_ge(vec_setup, 7)
            V.tensor_scalar(slot_base[:, :], slot_base_i[:, :], float(S), None, ALU.mult).then_inc(vec_setup, 1)
            dve.wait_ge(vec_setup, 8)
            dve.wait_ge(bias_loaded, 16 * 6)
            split_bias(V, slice(0, 2 * D), vec_split, bias_ready)
            dve.wait_ge(weights_ready, 2)

            def row_stats(src, side, done, count):
                for tt in range(TILES):
                    last = V.bn_stats(stats[:, side, tt, :], src[:, tt, :])
                last.then_inc(done, 1)
                dve.wait_ge(done, count)
                alone(dve)
                for tt in range(TILES):
                    last = V.bn_aggr(mv[:, side * TILES + tt, :], stats[:, side, tt, :])
                return last

            def step(at):
                x, a, c, r, t, f = at.x, at.a, at.c, at.r, at.t, at.f

                def next_indices(half):
                    if f is not None:
                        dve.wait_ge(gathered[half], f * 48 + 48)
                        alone(dve)
                    expert = bass.ds(at.next_expert + half, 1)
                    V.tensor_copy(gather_idx[:, half, :], tab_idx[at.next_group % 2][:, :, expert]
                                  .rearrange("p a e -> p (a e)")).then_inc(gather_idx_ready[half], 1)

                def make_tables(g):
                    if f is not None:
                        for ready in table_ready:
                            dve.wait_ge(ready, f)
                    dve.wait_ge(tab_transposed, g + 1)
                    tab = ps_q[:, 0:TILES * 2 * E].rearrange("p (a w e) -> p a w e", a=TILES, w=2)
                    V.tensor_copy(tab_idx[g % 2][:, :, :], tab[:, :, 0, :])
                    V.tensor_copy(tab_gate[g % 2][:, :, :], tab[:, :, 1, :]).then_inc(tab_ready, 1)
                    dve.wait_ge(tab_ready, g + 1)

                def top_k(n):
                    if at.top_first is not None:
                        g, op = at.top_first, n
                    elif at.top_last is not None:
                        g, op = at.top_last, 9 + n
                    else:
                        return
                    k = op // 3
                    top = top_val[:, 8 * k:8 * k + 8]
                    dve.wait_ge(t_vec, g * 18 + 1 + op)
                    if op == 17:
                        if g > 0:
                            dve.wait_ge(slots_stored, 16 * g)
                        V.tensor_scalar(slots[:, 0, :], top_idx[:, 0:CAP], slot_base[:, 0:1], None, ALU.add)
                        V.tensor_copy(slots[:, 1, :], top_val[:, 0:CAP]).then_inc(slots_ready, 1)
                    elif op % 3 == 0:
                        V.max(top, affT[:, :]).then_inc(t_vec, 1)
                    elif op % 3 == 1:
                        V.max_index(top_idx[:, 8 * k:8 * k + 8], top, affT[:, :]).then_inc(t_vec, 1)
                    else:
                        V.match_replace(affT[:, :], top, affT[:, :], -1.0).then_inc(t_vec, 1)

                def scatter_table(half):
                    if not first(f):
                        dve.wait_ge(scattered[half], f * 48)
                        dve.wait_ge(y_ready, f * 2 - 1 + half)
                        alone(dve)
                    expert = bass.ds(at.expert + half, 1)
                    V.tensor_copy(gate[:, half, :], tab_gate[at.f_group % 2][:, :, expert]
                                  .rearrange("p a e -> p (a e)"))
                    V.tensor_scalar(scatter_idx[:, half, :], tab_idx[at.f_group % 2][:, :, expert]
                                    .rearrange("p a e -> p (a e)"),
                                    float(at.f_group * G * S), None, ALU.add).then_inc(table_ready[half], 1)

                def gelu_argument(half):
                    dve.wait_ge(u_squared, f * 2 + half + 1)
                    V.scalar_tensor_tensor(gelu_in[half][:, :], u_sq[half][:, :], 1.0, u[half][:, :],
                                           ALU.add, ALU.mult).then_inc(gelu_in_ready, 1)

                def hidden(half):
                    dve.wait_ge(tanh_done, f * 2 + half + 1)
                    if not first(f):
                        dve.wait_ge(ffn2_done, f * 2 + half - 1)
                    V.scalar_tensor_tensor(hidT[half][:, :], tanh_out[half][:, :], 1.0, u[half][:, :],
                                           ALU.add, ALU.mult).then_inc(hid_ready, 1)

                def rsqrt(i):
                    if i:
                        dve.wait_ge(rsqrt_vec, at.j * 9 + i)
                    if i == 0:
                        ins = V.tensor_scalar(nv[:, :], mv[:, :, 1], EPS, -0.5, ALU.add, ALU.mult)
                    elif i == 1:
                        ins = V.tensor_scalar(rstd[:, :].bitcast(I32), nv[:, :].bitcast(I32), -0.5, RSQRT_MAGIC,
                                              ALU.mult, ALU.add)
                    elif i in (2, 6):
                        ins = V.tensor_tensor(sq[:, :], rstd[:, :], rstd[:, :], ALU.mult)
                    elif i in (3, 7):
                        ins = V.scalar_tensor_tensor(sq[:, :], sq[:, :], 1.0 if i == 3 else 3.375, nv[:, :],
                                                     ALU.mult, ALU.mult)
                    elif i == 4:
                        ins = V.scalar_tensor_tensor(sq[:, :], sq[:, :], 5.0 / 3.0, sq[:, :], ALU.add, ALU.mult)
                    else:
                        ins = V.scalar_tensor_tensor(rstd[:, :], sq[:, :], 1.25 if i == 5 else 2.25, rstd[:, :],
                                                     ALU.add, ALU.mult)
                    ins.then_inc(rsqrt_vec, 1)

                def normalise(src, dst, side):
                    for tt in range(TILES):
                        k = side * TILES + tt
                        last = V.tensor_scalar(dst[:, tt, :], src[:, tt, :], mv[:, k, 0:1], rstd[:, k:k + 1],
                                               ALU.subtract, ALU.mult)
                    return last

                norms = x is not None or c is not None
                logits = ps_v[:, SP:SP + TILES * E].rearrange("p (a e) -> p a e", a=TILES)

                def add_bias(tt):
                    bank, off = (ps_s[0], SO[tt]) if tt < 2 else (ps_s[1], 0)
                    if first(a) and tt == 0:
                        dve.wait_ge(pool_setup, 6)
                    dve.wait_ge(s_done, a * 2 + 1 + (tt == 2))
                    alone(dve)
                    return V.tensor_tensor_reduce(
                        out=probs[:, SO[tt]:SO[tt] + SW[tt]], in0=bank[:, off:off + SW[tt]],
                        in1=dist_bias[:, tt, 0:SW[tt]], scale=1.0, scalar=NEG, op0=ALU.add, op1=ALU.max,
                        accum_out=row_max[:, tt:tt + 1])

                if c is not None:
                    dve.wait_ge(h_kept, c + 1)
                    if not first(c):
                        dve.wait_ge(attn_added, c)
                    V.tensor_copy(hres[:, :, :], hnext[:, :, :]).then_inc(res_kept, 1)
                top_k(0)
                if c is not None:
                    dve.wait_ge(exp_done, c * 3 + 3)
                    V.reciprocal(row_inv[:, :], row_sum[:, :]).then_inc(c_vec, 1)
                if a is not None:
                    if c is not None:
                        dve.wait_ge(res_kept, c + 1)
                    V.tensor_copy(hnext[:, :, :], h[:, :, :]).then_inc(h_kept, 1)
                top_k(1)
                if r is not None:
                    dve.wait_ge(logits_done, r + 1)
                    V.tensor_reduce(r_max[:, :, 0], logits, AX_X, ALU.max).then_inc(r_vec, 1)
                top_k(2)
                if f is not None:
                    V.tensor_scalar(half_b1[:, :], b1T[:, bass.ds(at.expert, 2)], 0.5, None, ALU.mult) \
                        .then_inc(pair_ready, 1)
                if r is not None:
                    dve.wait_ge(r_vec, r * 3 + 1)
                    V.tensor_tensor(r_exp[:, :, :], logits, r_max[:, :, :].to_broadcast([P, TILES, E]),
                                    ALU.subtract).then_inc(logits_read, 1)
                top_k(3)
                if at.tables is not None:
                    make_tables(at.tables)
                if at.prepares:
                    next_indices(0)
                    next_indices(1)
                if x is not None:
                    dve.wait_ge(relu_done, x + 1)
                    alone(dve)
                    row_stats(h, 0, x_vec, x + 1).then_inc(x_stats, 1)
                top_k(4)
                if c is not None:
                    dve.wait_ge(pv_done, c + 1)
                    dve.wait_ge(res_kept, c + 1)
                    dve.wait_ge(c_vec, c * 3 + 1)
                    if not first(c):
                        dve.wait_ge(rows_stored, c * 64)
                    for tt in range(TILES):
                        last = V.scalar_tensor_tensor(h2[:, tt, :], ps_v[:, tt * P:(tt + 1) * P],
                                                      row_inv[:, tt:tt + 1], hres[:, tt, :], ALU.mult, ALU.add)
                    last.then_inc(attn_added, 1)
                top_k(5)
                if f is not None:
                    gelu_argument(0)
                if c is not None:
                    dve.wait_ge(attn_added, c + 1)
                    alone(dve)
                    row_stats(h2, 1, c_vec, c * 3 + 2).then_inc(c_vec, 1)
                top_k(6)
                if f is not None:
                    hidden(0)
                top_k(7)
                if norms:
                    if x is not None:
                        dve.wait_ge(x_stats, x + 1)
                    if c is not None:
                        dve.wait_ge(c_vec, c * 3 + 3)
                    rsqrt(0)
                if a is not None:
                    add_bias(0)
                top_k(8)
                if norms:
                    rsqrt(1)
                if f is not None:
                    gelu_argument(1)
                    scatter_table(0)
                if r is not None:
                    dve.wait_ge(r_exp_done, r + 1)
                    V.tensor_reduce(r_sum[:, :, 0], r_exp[:, :, :], AX_X, ALU.add).then_inc(r_vec, 1)
                if norms:
                    rsqrt(2)
                if a is not None:
                    add_bias(1)
                if norms:
                    rsqrt(3)
                    rsqrt(4)
                if a is not None:
                    add_bias(2).then_inc(a_vec, 1)
                if norms:
                    rsqrt(5)
                if a is not None:
                    dve.wait_ge(a_vec, a + 1)
                    V.tensor_scalar(neg_max[:, :], row_max[:, :], -1.0, None, ALU.mult).then_inc(max_ready, 1)
                if f is not None:
                    hidden(1)
                if norms:
                    rsqrt(6)
                    rsqrt(7)
                    rsqrt(8)
                if c is not None:
                    dve.wait_ge(rsqrt_vec, at.j * 9 + 9)
                    if not first(c):
                        dve.wait_ge(xn2_transposed, c)
                    normalise(h2, xn2, 1).then_inc(xn2_ready, 1)
                if r is not None:
                    dve.wait_ge(r_vec, r * 3 + 2)
                    V.reciprocal(r_sum[:, :, :], r_sum[:, :, :]).then_inc(r_vec, 1)
                    dve.wait_ge(r_vec, r * 3 + 3)
                    V.tensor_tensor(aff[:, :, :, bass.ds(at.r_in_group, 1)].rearrange("p a e g -> p a (e g)"),
                                    r_exp[:, :, :], r_sum[:, :, :].to_broadcast([P, TILES, E]), ALU.mult) \
                        .then_inc(aff_ready, 1)
                if f is not None:
                    scatter_table(1)
                if x is not None:
                    dve.wait_ge(rsqrt_vec, at.j * 9 + 9)
                    if not first(x):
                        dve.wait_ge(xn_transposed, x)
                    normalise(h, xn, 0).then_inc(xn_ready, 1)
                if t is not None:
                    dve.wait_ge(aff_transposed, t + 1)
                    V.tensor_copy(affT[:, :], ps_s[1][:, 0:S]).then_inc(t_vec, 1)

            steps(dve, step)


_INS = ["x", "L0_tok_weight", "L0_tok_bias", "L0_attn_W_qk", "L0_attn_W_v", "L0_attn_b_v", "L0_ffn_gate_weight",
        "L0_ffn_w1", "L0_ffn_b1", "L0_ffn_w2", "L0_ffn_b2"]


def kernel(**inputs):
    import numpy as _np
    import concourse.bacc as _bacc
    from concourse import mybir as _mybir
    from concourse.bass_utils import run_bass_kernel_spmd as _run

    nc = _bacc.Bacc("TRN2", target_bir_lowering=False, num_devices=1)
    arrays, args = {}, []
    for name in _INS:
        a = _np.ascontiguousarray(inputs[name])
        arrays[f"in_{name}"] = a
        args.append(nc.dram_tensor(f"in_{name}", a.shape, _mybir.dt.from_np(a.dtype), kind="ExternalInput").ap())
    batch, tokens, d = inputs["x"].shape
    rows = tokens - inputs["L0_tok_weight"].shape[1] // d + 1
    experts = inputs["L0_ffn_gate_weight"].shape[1]
    f32 = _mybir.dt.float32
    out = nc.dram_tensor("out_0", (batch, rows, d), f32, kind="ExternalOutput").ap()
    group = 128 // experts
    xn2_rows = [nc.dram_tensor(f"xn2_rows_{i}", (group * rows, d), f32).ap() for i in range(batch // group)]
    slots_dram = nc.dram_tensor("slots_scratch", (2, 128, rows // experts * 2), f32).ap()
    audio_tower_block(nc, *args, out, xn2_rows, slots_dram)
    r = _run(nc, [arrays], core_ids=[0])
    return r.results[0]["out_0"]
```
